# Optimizing a Trainium2 kernel written in Bass

```python
import numpy as np
import jax
import jax.numpy as jnp

def _softmax(x, axis=-1):
    return jax.nn.softmax(x, axis=axis)

def _gelu(x):
    return jax.nn.gelu(x, approximate=True)

def _silu(x):
    return jax.nn.silu(x)

def _sigmoid(x):
    return jax.nn.sigmoid(x)

def _layernorm(x, axis=-1, eps=1e-05):
    m = jnp.mean(x, axis=axis, keepdims=True)
    v = jnp.var(x, axis=axis, keepdims=True)
    return (x - m) / jnp.sqrt(v + eps)

def _scatter_add(tgt, idx, src, axis=0):
    return tgt.at[idx].add(src)

def _segment_sum(src, seg, n):
    return jax.ops.segment_sum(src, seg, n)
kernel_name = 'mk_gnn_preln_d4_gnn_r16_ca5f5a'

def setup_inputs(seed: int=0):
    np.random.seed(seed)
    _w = jnp.asarray

    def _rec_inputs():
        import jax
        import jax.numpy as jnp
        _gk = jax.random.key(seed)
        x = -0.000202 + 1 * jax.random.normal(jax.random.fold_in(_gk, 1), (6250, 128), jnp.float32)
        _s = jax.random.randint(jax.random.fold_in(_gk, 2), (100000,), 0, 6250, jnp.int32)
        _d = jax.random.randint(jax.random.fold_in(_gk, 3), (100000,), 0, 6250, jnp.int32)
        _loop = jnp.arange(6250, dtype=jnp.int32)
        src = jnp.concatenate([_s, _d, _loop])
        dst = jnp.concatenate([_d, _s, _loop])
        _o = jnp.argsort(dst, stable=True)
        src = src[_o]
        dst = dst[_o]
        edge_attr_10 = 0.000254407 + 0.99978 * jax.random.normal(jax.random.fold_in(_gk, 11), (206250, 10), jnp.float32)
        edge_weight = jax.random.uniform(jax.random.fold_in(_gk, 13), (206250,), jnp.float32, 0.0, 0.999999)
        return (x, src, dst, edge_attr_10, edge_weight)
    x, src, dst, edge_attr_10, edge_weight = _rec_inputs()

    def _L0_gnn_setup():
        import jax, jax.numpy as jnp
        import numpy as np
        N_NODES = 3125
        N_EDGES = 50000
        C_IN = 128
        C_OUT = 128
        BN_EPS = 1e-05
        key = jax.random.key(seed)
        k1, k2, k3 = jax.random.split(key, 3)
        x = jax.random.normal(k1, (N_NODES, C_IN), dtype=jnp.float32)
        edge_index = jax.random.randint(k2, (2, N_EDGES), 0, N_NODES, dtype=jnp.int64)
        weight = jax.random.normal(k3, (C_IN, C_OUT), dtype=jnp.float32) * (1.0 / np.sqrt(C_IN))
        bias = jnp.zeros((C_OUT,), dtype=jnp.float32)
        gamma = jnp.ones((C_OUT,), dtype=jnp.float32)
        beta = jnp.zeros((C_OUT,), dtype=jnp.float32)
        return {'x': x, 'edge_index': edge_index, 'weight': weight, 'bias': bias, 'gamma': gamma, 'beta': beta}
    _L0_gnn_all = _L0_gnn_setup()
    _L0_gnn_in = {k: v for k, v in _L0_gnn_all.items() if k in ('weight', 'bias', 'gamma', 'beta')}
    del _L0_gnn_all

    def _L1_gnn_setup():
        import jax, jax.numpy as jnp
        import numpy as np
        N_NODES = 3125
        N_EDGES = 50000
        IN_DIM = 128
        HID = 128
        EDGE_DIM = 10
        BN_EPS = 1e-05
        key = jax.random.key(seed)
        ks = jax.random.split(key, 12)
        s = 0.05
        return {'x': jax.random.normal(ks[0], (N_NODES, IN_DIM), dtype=jnp.float32), 'edge_index': jax.random.randint(ks[1], (2, N_EDGES), 0, N_NODES, dtype=jnp.int32), 'edge_attr': jax.random.normal(ks[2], (N_EDGES, EDGE_DIM), dtype=jnp.float32), 'Wq': jax.random.normal(ks[3], (HID, IN_DIM), dtype=jnp.float32) * s, 'bq': jnp.zeros((HID,), dtype=jnp.float32), 'Wk': jax.random.normal(ks[4], (HID, IN_DIM), dtype=jnp.float32) * s, 'bk': jnp.zeros((HID,), dtype=jnp.float32), 'Wv': jax.random.normal(ks[5], (HID, IN_DIM), dtype=jnp.float32) * s, 'bv': jnp.zeros((HID,), dtype=jnp.float32), 'We': jax.random.normal(ks[6], (HID, EDGE_DIM), dtype=jnp.float32) * s, 'Wskip': jax.random.normal(ks[7], (HID, IN_DIM), dtype=jnp.float32) * s, 'bskip': jnp.zeros((HID,), dtype=jnp.float32), 'gamma': jnp.ones((HID,), dtype=jnp.float32), 'beta': jnp.zeros((HID,), dtype=jnp.float32)}
    _L1_gnn_all = _L1_gnn_setup()
    _L1_gnn_in = {k: v for k, v in _L1_gnn_all.items() if k in ('Wq', 'bq', 'Wk', 'bk', 'Wv', 'bv', 'We', 'Wskip', 'bskip', 'gamma', 'beta')}
    del _L1_gnn_all

    def _L2_gnn_setup():
        import jax, jax.numpy as jnp
        import numpy as np
        N_NODES = 6250
        N_EDGES = 100000
        D_IN = 128
        D_OUT = 128
        key = jax.random.key(seed)
        k1, k2, k3, k4 = jax.random.split(key, 4)
        X = jax.random.normal(k1, (N_NODES, D_IN), dtype=jnp.float32)
        edge_index = jax.random.randint(k2, (2, N_EDGES), 0, N_NODES, dtype=jnp.int32)
        edge_values = jax.random.uniform(k3, (N_EDGES,), dtype=jnp.float32)
        W = jax.random.normal(k4, (D_OUT, D_IN), dtype=jnp.float32) * 0.01
        b = jnp.zeros((D_OUT,), dtype=jnp.float32)
        return {'X': X, 'edge_index': edge_index, 'edge_values': edge_values, 'W': W, 'b': b}
    _L2_gnn_all = _L2_gnn_setup()
    _L2_gnn_in = {k: v for k, v in _L2_gnn_all.items() if k in ('W', 'b')}
    del _L2_gnn_all

    def _L3_gnn_setup():
        import jax, jax.numpy as jnp
        import numpy as np
        N_NODES = 6250
        N_EDGES = 40000
        D_FEAT = 128
        key = jax.random.key(seed)
        k1, k2, k3, k4 = jax.random.split(key, 4)
        x = jax.random.normal(k1, (N_NODES, D_FEAT), dtype=jnp.float32)
        edge_index = jax.random.randint(k2, (2, N_EDGES), 0, N_NODES, dtype=jnp.int64)
        W = jax.random.normal(k3, (D_FEAT, D_FEAT), dtype=jnp.float32) / np.sqrt(D_FEAT)
        W_self = jax.random.normal(k4, (D_FEAT, D_FEAT), dtype=jnp.float32) / np.sqrt(D_FEAT)
        return {'x': x, 'edge_index': edge_index, 'W': W, 'W_self': W_self}
    _L3_gnn_all = _L3_gnn_setup()
    _L3_gnn_in = {k: v for k, v in _L3_gnn_all.items() if k in ('W', 'W_self')}
    del _L3_gnn_all
    return {'x': x, 'src': src, 'dst': dst, 'edge_attr_10': edge_attr_10, 'edge_weight': edge_weight, 'L0_gnn_weight': _L0_gnn_in['weight'], 'L0_gnn_bias': _L0_gnn_in['bias'], 'L0_gnn_gamma': _L0_gnn_in['gamma'], 'L0_gnn_beta': _L0_gnn_in['beta'], 'L1_gnn_Wq': _L1_gnn_in['Wq'], 'L1_gnn_bq': _L1_gnn_in['bq'], 'L1_gnn_Wk': _L1_gnn_in['Wk'], 'L1_gnn_bk': _L1_gnn_in['bk'], 'L1_gnn_Wv': _L1_gnn_in['Wv'], 'L1_gnn_bv': _L1_gnn_in['bv'], 'L1_gnn_We': _L1_gnn_in['We'], 'L1_gnn_Wskip': _L1_gnn_in['Wskip'], 'L1_gnn_bskip': _L1_gnn_in['bskip'], 'L1_gnn_gamma': _L1_gnn_in['gamma'], 'L1_gnn_beta': _L1_gnn_in['beta'], 'L2_gnn_W': _L2_gnn_in['W'], 'L2_gnn_b': _L2_gnn_in['b'], 'L3_gnn_W': _L3_gnn_in['W'], 'L3_gnn_W_self': _L3_gnn_in['W_self']}

def reference(x, src, dst, edge_attr_10, edge_weight, L0_gnn_weight, L0_gnn_bias, L0_gnn_gamma, L0_gnn_beta, L1_gnn_Wq, L1_gnn_bq, L1_gnn_Wk, L1_gnn_bk, L1_gnn_Wv, L1_gnn_bv, L1_gnn_We, L1_gnn_Wskip, L1_gnn_bskip, L1_gnn_gamma, L1_gnn_beta, L2_gnn_W, L2_gnn_b, L3_gnn_W, L3_gnn_W_self):
    import jax
    import jax.numpy as jnp

    def _L0_gnn_ref(x, edge_index, weight, bias, gamma, beta):
        import jax, jax.numpy as jnp
        import numpy as np
        N_NODES = 3125
        N_EDGES = 50000
        C_IN = 128
        C_OUT = 128
        BN_EPS = 1e-05
        'GNNBlock forward: GCNConv -> BatchNorm1d (batch stats) -> ReLU.\n            Dropout is identity in eval / deterministic reference.'
        n = x.shape[0]
        src, dst = (edge_index[0], edge_index[1])
        xw = x @ weight
        ones = jnp.ones((src.shape[0],), dtype=x.dtype)
        deg = jax.ops.segment_sum(ones, dst, num_segments=n) + 1.0
        dinv = jax.lax.rsqrt(deg)
        norm = dinv[src] * dinv[dst]
        msg = xw[src] * norm[:, None]
        agg = jax.ops.segment_sum(msg, dst, num_segments=n)
        agg = agg + xw * (dinv * dinv)[:, None]
        agg = agg + bias
        mean = jnp.mean(agg, axis=0)
        var = jnp.mean(jnp.square(agg - mean), axis=0)
        h = (agg - mean) * jax.lax.rsqrt(var + BN_EPS) * gamma + beta
        return jax.nn.relu(h)

    def _L1_gnn_ref(x, edge_index, edge_attr, Wq, bq, Wk, bk, Wv, bv, We, Wskip, bskip, gamma, beta):
        import jax, jax.numpy as jnp
        import numpy as np
        N_NODES = 3125
        N_EDGES = 50000
        IN_DIM = 128
        HID = 128
        EDGE_DIM = 10
        BN_EPS = 1e-05
        N = x.shape[0]
        d = Wq.shape[0]
        src, dst = (edge_index[0], edge_index[1])
        q_all = x @ Wq.T + bq
        k_all = x @ Wk.T + bk
        v_all = x @ Wv.T + bv
        e = edge_attr @ We.T
        q = q_all[dst]
        k = k_all[src] + e
        v = v_all[src] + e
        scale = 1.0 / jnp.sqrt(jnp.asarray(d, dtype=x.dtype))
        alpha = (q * k).sum(-1) * scale
        amax = jax.ops.segment_max(alpha, dst, num_segments=N)
        ex = jnp.exp(alpha - amax[dst])
        denom = jax.ops.segment_sum(ex, dst, num_segments=N)
        w = ex / denom[dst]
        agg = jax.ops.segment_sum(v * w[:, None], dst, num_segments=N)
        out = agg + x @ Wskip.T + bskip
        h = jax.nn.relu(out)
        mean = h.mean(0)
        var = ((h - mean) ** 2).mean(0)
        return gamma * (h - mean) * jax.lax.rsqrt(var + BN_EPS) + beta

    def _L2_gnn_ref(X, edge_index, edge_values, W, b):
        import jax, jax.numpy as jnp
        import numpy as np
        N_NODES = 6250
        N_EDGES = 100000
        D_IN = 128
        D_OUT = 128
        dst = edge_index[0]
        src = edge_index[1]
        msgs = edge_values[:, None] * X[src]
        AX = jax.ops.segment_sum(msgs, dst, num_segments=X.shape[0])
        return jnp.einsum('nd,od->no', AX, W) + b

    def _L3_gnn_ref(x, edge_index, W, W_self):
        import jax, jax.numpy as jnp
        import numpy as np
        N_NODES = 6250
        N_EDGES = 40000
        D_FEAT = 128
        src = edge_index[0]
        tgt = edge_index[1]
        messages = jnp.take(x, src, axis=0) @ W
        aggr_out = jax.ops.segment_sum(messages, tgt, num_segments=x.shape[0])
        return aggr_out + x @ W_self
    edge_index = jnp.stack([src, dst])
    h = jnp.maximum(_layernorm(x, axis=-1), 0.0)
    x = x + _L0_gnn_ref(h, edge_index, L0_gnn_weight, L0_gnn_bias, L0_gnn_gamma, L0_gnn_beta)
    h = jnp.maximum(_layernorm(x, axis=-1), 0.0)
    x = x + _L1_gnn_ref(h, edge_index, edge_attr_10, L1_gnn_Wq, L1_gnn_bq, L1_gnn_Wk, L1_gnn_bk, L1_gnn_Wv, L1_gnn_bv, L1_gnn_We, L1_gnn_Wskip, L1_gnn_bskip, L1_gnn_gamma, L1_gnn_beta)
    h = jnp.maximum(_layernorm(x, axis=-1), 0.0)
    x = x + _L2_gnn_ref(h, edge_index, edge_weight, L2_gnn_W, L2_gnn_b)
    h = jnp.maximum(_layernorm(x, axis=-1), 0.0)
    x = x + _L3_gnn_ref(h, edge_index, L3_gnn_W, L3_gnn_W_self)
    return x

_drawn_inputs = setup_inputs


def setup_inputs(seed=0):
    import zlib

    import numpy as np

    out = dict(_drawn_inputs(seed))
    spreads = {'L0_gnn_bias': (0.0, 2.0),
     'L0_gnn_gamma': (1.0, 0.2),
     'L0_gnn_beta': (0.0, 0.1),
     'L1_gnn_bq': (0.0, 0.8),
     'L1_gnn_bk': (0.0, 2.0),
     'L1_gnn_bv': (0.0, 0.316),
     'L1_gnn_bskip': (0.0, 0.345),
     'L1_gnn_gamma': (1.0, 0.2),
     'L1_gnn_beta': (0.0, 0.1),
     'L2_gnn_b': (0.0, 0.1)}
    factors = {'L1_gnn_Wq': 6.312, 'L1_gnn_Wk': 6.992}
    for name, (base, spread) in spreads.items():
        noise = np.random.default_rng([zlib.crc32(name.encode()), seed]).standard_normal(out[name].shape)
        drawn = base * np.exp(spread * noise) if base else spread * noise
        out[name] = jnp.asarray(drawn.astype(out[name].dtype))
    for name, factor in factors.items():
        out[name] = (out[name] * factor).astype(out[name].dtype)
    return out
```

```python
from contextlib import ExitStack

import concourse.bass as bass
from concourse import mybir

f32, bf16, i32, i16 = mybir.dt.float32, mybir.dt.bfloat16, mybir.dt.int32, mybir.dt.int16
ALU = mybir.AluOpType
ACT = mybir.ActivationFunctionType
AX = mybir.AxisListType
ENG = mybir.EngineType

P = 128
CH = 16
GR = 4
TABLES = 8
MASKED = 1.0e30
NOTHING = 1.0e29
LN_EPS = BN_EPS = 1e-5


def gnn_kernel(nc, x, src, dst, ea, ew, w0, b0, g0, be0, wq, bq, wk, bk, wv, bv, we, wskip, bskip,
               g1, be1, w2, b2, w3, wself, out):
    N, F = x.shape
    E = src.shape[0]
    ED = ea.shape[1]
    assert F == P
    W = (N + P - 1) // P
    NP = W * P
    T = (E + P - 1) // P
    PB = (T + W - 1 + P - 1) // P
    PC = PB * P
    NCH = PC // CH
    assert NCH % 2 == 0
    X1 = 1 + ED
    FX = F + X1
    SCALE = float(F) ** -0.5
    FAR = 1 << 13
    assert FAR >= NP + P
    FULL = N // P
    REST = N - FULL * P
    BLK = [(b, min(4, W - b)) for b in range(0, W, 4)]
    NB = len(BLK)
    QB = [(b, min(3, W - b)) for b in range(0, W, 3)]
    NQ = len(QB)

    def dram(name, shape, dt):
        return nc.dram_tensor(name, shape, dt).ap()

    src_t, dst_all = dram("src_tiles", [PC, P], i32), dram("dst_tiles", [PC + 1, P], i32)
    dst_t = dst_all[0:PC, :]
    ew_t, ea_t = dram("weight_tiles", [PC, P], f32), dram("attr_tiles", [PC, P * ED], f32)
    ea_p = dram("attr_pairs", [PC, P * ED], f32)
    src_p = dram("src_pairs", [PC, P], f32)
    loc_p = dram("local_dst_pairs", [PC, P], bf16)
    win_d = dram("window_of_pair", [PC, 1], i16)
    ew_pc = dram("weight_columns", [P, PC], f32)
    table = [dram(f"gather_table{l}", [NP, F], f32) for l in range(3)]
    sums = [dram(f"scattered_sums{k}", [NP + P, F], f32) for k in range(TABLES)]

    ctx = ExitStack()
    with ctx:
        def sb(name, shape, dt=f32):
            return ctx.enter_context(nc.sbuf_tensor(name, shape, dt))

        def sem(name):
            return ctx.enter_context(nc.semaphore(name))

        X = sb("X", [P, W, F])
        NH = max(W * F, CH * FX + CH * P + 8 * P + 2 * GR * P)
        NR1 = max((3 * W * FX + 1) // 2, 5 * CH * P, 5 * PC, 2 * TABLES * 4 * P)
        hflat = sb("H", [P, NH])[:, :]
        H = hflat[:, 0:W * F].rearrange("p (w f) -> p w f", f=F)
        HT = sb("HT", [P, max(NP, 2 * P * ED + PC, 2 * PC, 3 * CH * P)])[:, :]
        accflat = sb("ACC", [P, max(W * FX, 2 * PC)])[:, :]
        ACC = accflat[:, 0:W * FX].rearrange("p (w f) -> p w f", f=FX)
        r1 = sb("R1", [P, NR1])[:, :]
        R2 = sb("R2", [P, 2 * CH * P], f32)
        G = sb("G", [P, CH, FX])
        loc_c = sb("loc_c", [P, PC])
        idx_c = sb("idx_c", [P, PC], i32)
        win = sb("win", [1, PC], i16)
        idx_f = sb("idx_f", [P, 2, CH], i32)
        col_f = sb("col_f", [P, 2, 3, CH])
        aux_c = sb("aux_c", [P, PC])
        att = sb("att", [P, 5, CH])
        iota_i = sb("iota_i", [P, P], i32)
        iota_p = sb("iota_p", [P, 1], i32)
        iota = sb("iota", [P, P])
        row = sb("row", [P, 1])
        ident = sb("ident", [P, P])
        ident_b = sb("ident_b", [P, P], bf16)
        ones = sb("ones", [P, P])
        ones_b = sb("ones_b", [P, 1], bf16)
        zeros = sb("zeros", [P, P])
        far = sb("far", [P, P], i32)
        dinv = sb("dinv", [P, W])
        lns = sb("lns", [P, 4, W])
        bns = sb("bns", [P, 8])
        cols = sb("cols", [P, 8])
        b2row = sb("b2row", [1, F])
        Wm = sb("Wm", [P, 7, P])
        WT = sb("WT", [P, 4, P])
        C = sb("C", [P, FX])
        VX = sb("VX", [P, X1])
        VXT = sb("VXT", [X1, P])

        r2b = R2[:, :].bitcast(bf16)

        def pairs(ap):
            return ap.rearrange("p (b e) -> p b e", e=P)

        rows_src, rows_dst, rows_ew = (pairs(r1[:, k * PC:(k + 1) * PC]) for k in range(3))
        rows_locb = pairs(r1[:, 3 * PC:3 * PC + PC // 2].bitcast(bf16))
        tile_dst = pairs(accflat[:, 0:PC])
        rows_loc = pairs(accflat[:, PC:2 * PC])
        rows_ea = HT[:, 0:2 * P * ED].rearrange("p (u a) -> p u a", u=2)
        ew_cols = r1[:, 4 * PC:5 * PC]
        rows_srcf = pairs(HT[:, 2 * P * ED:2 * P * ED + PC])
        prep = sb("prep", [P, 4 * PB + 3 * (W - 1)])
        last, pair, wof, negw = (prep[:, i * PB:(i + 1) * PB] for i in range(4))
        K1 = W - 1
        thr, cnt_k, bnd = (prep[:, 4 * PB + i * K1:4 * PB + (i + 1) * K1] for i in range(3))
        toff = sb("toff", [P, PB], i32)
        wofi = sb("wofi", [P, PB], i16)
        dst_l, next_l, place = (r1[:, k * PC:(k + 1) * PC].bitcast(i32) for k in range(3))
        hi, mask = (r1[:, k * PC:(k + 1) * PC] for k in range(3, 5))
        src_l, ew_l = accflat[:, 0:PC].bitcast(i32), accflat[:, PC:2 * PC]
        placef, ranks = HT[:, 0:PC], HT[:, PC:2 * PC]
        W1 = W + 1
        upper = R2[:, 0:P]
        in_window, before_window, starts = (R2[:, P + k * W1:P + (k + 1) * W1] for k in range(3))
        number, count, total, start, order = (R2[:, P + 3 * W1 + k:P + 3 * W1 + k + 1] for k in range(5))
        at = P + 3 * W1 + 5
        attr_s = R2[:, at:at + CH * ED].rearrange("p (c a) -> p c a", a=ED)
        at += CH * ED
        place_s, src_s, dst_s = (R2[:, at + k * CH:at + (k + 1) * CH].bitcast(i32) for k in range(3))
        ew_s = R2[:, at + 3 * CH:at + 4 * CH]
        cmp_k = R2[:, 0:K1 * PB].rearrange("p (k b) -> p k b", b=PB)
        cmp_p = R2[:, 0:K1 * PB].rearrange("p (b k) -> p b k", k=K1)
        counts = r1[:, 0:PC]
        counts_t = pairs(r1[:, PC:2 * PC])
        selector = r1[:, 2 * PC:2 * PC + PB * W].rearrange("p (b w) -> p b w", w=W)
        onehot = R2[:, :].rearrange("p (u j n) -> p u j n", u=2, j=CH)
        onehot_b = r2b[:, 0:2 * CH * P].rearrange("p (u j n) -> p u j n", u=2, j=CH)
        G_plain = [G[:, :, :], r1[:, 0:CH * FX].rearrange("p (j f) -> p j f", f=FX)]
        Q3 = r1.bitcast(bf16)[:, 0:3 * W * FX].rearrange("p (t w f) -> p t w f", t=3, w=W)
        QT = accflat[:, 0:NP]
        member = r2b[:, 0:2 * CH * P].rearrange("p (u j e) -> p u j e", u=2, j=CH)
        penalty = r2b[:, 2 * CH * P:4 * CH * P].rearrange("p (u j e) -> p u j e", u=2, j=CH)
        G_att = [G[:, :, :], hflat[:, 0:CH * FX].rearrange("p (j f) -> p j f", f=FX)]
        at = CH * FX
        locrow = hflat[:, at:at + CH * P].bitcast(bf16).rearrange("p (u m) -> p u m", u=2)
        at += CH * P
        Eb = hflat[:, at:at + 2 * P].rearrange("p (j e) -> p j e", e=P)
        at += 2 * P
        ET = hflat[:, at:at + 4 * P].rearrange("p (j n) -> p j n", n=P)
        at += 4 * P
        masked = hflat[:, at:at + 2 * P].rearrange("p (j e) -> p j e", e=P)
        at += 2 * P
        ST = hflat[:, at:at + P].bitcast(bf16)[0:3 * GR, :].rearrange("r (g e) -> r g e", g=2)
        at += P
        pick = hflat[:, at:at + GR * P // 2].bitcast(bf16)[0:3 * GR, :].rearrange("r (j n) -> r j n", j=GR)
        at += GR * P // 2
        assert at <= NH
        winrow = R2[:, 0:PC // 2].bitcast(i16)
        qrem = R2[:, 0:6 * FX].rearrange("p (i f) -> p i f", f=FX)
        EXT = r1[0:X1, 0:NP]
        srcrow = r1[:, 0:2 * CH * P].rearrange("p (u m) -> p u m", u=2)
        same = r1[:, 2 * CH * P:4 * CH * P].rearrange("p (u j e) -> p u j e", u=2, j=CH)
        cmb = r1[:, 4 * CH * P:5 * CH * P].rearrange("p (j e) -> p j e", e=P)
        ysc = HT[:, 0:2 * CH * P].rearrange("p (u j f) -> p u j f", u=2, j=CH)
        earlier = HT[:, 2 * CH * P:3 * CH * P].rearrange("p (j e) -> p j e", e=P)
        blkbuf = r1[:, 0:2 * TABLES * 4 * P].rearrange("p (u k w f) -> p u k w f", u=2, k=TABLES, w=4)
        H3T = r1[:, 0:NP]
        AGT = hflat[:, 0:NP]
        unordered = sb("unordered", [P, 1], i32)
        dump = sb("dump", [P, 1])
        junk = sb("junk", [P, 2, FX])
        parts = sb("parts", [P, 2, 3 * GR], bf16)
        rem_s = sb("rem_s", [P, 2, GR])
        picks = sb("picks", [P, GR])
        lower = sb("lower", [P, P])

        psum = ctx.enter_context(nc.psum_tensor("psum", [P, 8, 512], f32))

        rows_ps = psum[0:3 * GR, 4, P:P + P // 2].bitcast(bf16)

        def bank4(b):
            return psum[:, b, :].rearrange("p (k f) -> p k f", f=P)

        def dep(s):
            return psum[:, s // 3, (s % 3) * FX:(s % 3 + 1) * FX]

        s_w = sem("weights_loaded")
        s_wt = sem("weights_transposed")
        s_wtc = sem("transposed_weights_copied")
        s_x = sem("x_loaded")
        s_iota = sem("iota_written")
        s_const = sem("constants_written")
        s_pad = sem("edge_tables_filled")
        s_lin = sem("linear_edges_loaded")
        s_cmp = sem("orders_compared")
        s_cmps = sem("orders_summed")
        s_flag = sem("order_known")
        s_cw = sem("edges_of_windows_counted")
        s_cws = sem("starts_of_windows_summed")
        s_place = sem("places_known")
        s_vp = sem("placing_step")
        s_copy = sem("attributes_set_aside")
        s_stage = sem("records_loaded")
        s_take = sem("records_copied")
        s_taken = sem("records_claimed")
        s_put = sem("records_placed")
        s_order = sem("edge_tables_in_order")
        s_tdst = sem("tile_dst_loaded")
        s_cntk = sem("boundaries_counted")
        s_aps = sem("boundaries_summed")
        s_toff = sem("tile_of_pair_known")
        s_rows = sem("pair_rows_gathered")
        s_eag = [sem("attr_rows_gathered0"), sem("attr_rows_gathered1")]
        s_eaw = [sem("attr_rows_stored0"), sem("attr_rows_stored1")]
        s_loc = sem("pair_rows_are_numbers")
        s_pw = sem("pair_rows_stored")
        s_win = sem("window_row_loaded")
        s_pt = sem("pair_rows_transposed")
        s_pta = sem("pair_columns_copied_by_scalar")
        s_ptd = sem("pair_columns_copied_by_vector")
        s_ewp = sem("weight_columns_stored")
        s_d = sem("vector_step")
        s_oh = sem("one_hots_written")
        s_dm = sem("pair_counted")
        s_dmc = sem("pair_count_copied")
        s_ct = sem("counts_transposed")
        s_ctc = sem("transposed_counts_copied")
        s_sel = sem("selectors_written")
        s_deg = sem("degrees_summed")
        s_dg = sem("degrees_in_sbuf")
        s_dgr = sem("degree_roots")
        s_ln0 = sem("first_norm_done")
        s_lnc = sem("rows_centred")
        s_lnq = sem("rows_squared")
        s_lnv = sem("row_variances")
        s_lns = sem("row_deviations")
        s_h = sem("h_ready")
        s_tab = [sem(f"gather_table{l}_stored") for l in range(3)]
        s_zero = sem("scattered_sums_zeroed")
        s_g = [sem(f"rows_gathered{k}") for k in range(8)]
        s_idx = sem("indices_placed")
        s_claim = sem("group_claimed")
        s_use = sem("rows_used")
        s_add = sem("pair_added")
        s_z = sem("sums_ready")
        s_tr = sem("block_transposed")
        s_trc = sem("block_copied")
        s_mo = sem("block_product")
        s_moc = sem("block_product_used")
        s_bnc = sem("columns_centred")
        s_bnq = sem("columns_squared")
        s_bnv = sem("column_variance")
        s_bns = sem("column_deviation")
        s_bna = sem("column_scale")
        s_bn = sem("columns_normalised")
        s_bt = sem("block_transposed_back")
        s_btc = sem("block_added_to_x")
        s_wrow = sem("window_rows_loaded")
        s_aux = sem("weight_columns_loaded")
        s_q = sem("queries_product")
        s_qh = sem("queries_high_part")
        s_qs = sem("queries_split")
        s_att = sem("attention_ready")
        s_lr = [sem("local_rows_loaded0"), sem("local_rows_loaded1")]
        s_ea = [sem("attrs_loaded0"), sem("attrs_loaded1")]
        s_mem = sem("members_written")
        s_qe = sem("queries_spread")
        s_dot = sem("score_ready")
        s_shi = sem("scores_high_part")
        s_srem = sem("scores_remainder")
        s_smid = sem("scores_middle_part")
        s_slo = sem("scores_low_part")
        s_str = sem("score_parts_transposed")
        s_stc = sem("score_rows_copied")
        s_row = sem("scores_as_row")
        s_nmo = sem("old_maximum_ready")
        s_min = sem("new_maximum_ready")
        s_exp = sem("exponentials_ready") 
        s_c = sem("correction_ready")
        s_et = sem("exponentials_transposed")    
        s_etc = sem("exponentials_copied")       
        s_acc = sem("attention_added")    
        s_agn = sem("attention_normalised")
        s_sr = [sem("src_rows_loaded0"), sem("src_rows_loaded1")]
        s_m2 = sem("same_and_weighted_written")
        s_col = sem("columns_placed")
        s_same = sem("equal_src_written")
        s_ear = sem("earlier_edges_written")
        s_small = sem("duplicates_step")
        s_cm = sem("combination_ready")
        s_cmc = sem("combination_copied")
        s_y = sem("rows_to_scatter_ready")
        s_yc = sem("rows_to_scatter_copied")
        s_ix2 = sem("scatter_indices_ready")
        s_clm2 = sem("scatter_claimed")
        s_sc = [sem(f"scattered{k}") for k in range(TABLES)]
        s_bl = [sem("sum_blocks_loaded0"), sem("sum_blocks_loaded1")]
        s_out = sem("output_stored")

        block = ctx.enter_context(nc.Block())

        TAIL = T * P - E
        assert 0 < TAIL and 0 < REST
        fills = []
        for t, fill, m, end in ((src_t, zeros[:, :].bitcast(i32), 1, PC), (dst_all, far[:, :], 1, PC + 1),
                                (ew_t, zeros[:, :], 1, PC), (ea_t, zeros[:, :], ED, PC)):
            width = P * m
            for r0, r1_, c0 in [(T - 1, T, (P - TAIL) * m)] + [(r, min(r + P, end), 0) for r in range(T, end, P)]:
                for c in range(c0, width, P):
                    n = min(P, width - c)
                    fills.append((t[r0:r1_, c:c + n], fill[0:r1_ - r0, 0:n]))
        WEIGHTS = 16 * (7 + 1 + 9 + 3)
        PADS = 16 * (4 + len(fills))

        def load_windows(eng, first, n):
            return nc.values_load_multi_w_load_instructions(
                win[0:1, bass.ds(first, n)], engines=[eng], min_val=0, max_val=W - 1,
                skip_runtime_bounds_check_because="a count of at most W - 1 boundaries")[1]

        def load_flag(eng):
            return nc.values_load_multi_w_load_instructions(
                unordered[0:1, 0:1], engines=[eng], min_val=0, max_val=P,
                skip_runtime_bounds_check_because="a count of partitions")[1][0]

        LAST = 12
        TURNS = (PC - LAST - 33) // 32 + 1
        assert PC >= 64

        def there(i, k):
            return not isinstance(i, int) or 0 <= i + k < PC

        def attention(eng, body):
            for k in range(-4, LAST):
                body(0, k)
            with eng.Fori(0, 32 * (TURNS - 1) + 1, 32) as i:
                for k in range(LAST, LAST + 32):
                    body(i, k)
            for k in range(LAST, PC + LAST - 32 * TURNS):
                body(32 * TURNS, k)

        def loop(eng, body, n, *args, first=0):
            with eng.Fori(first, n - 2 * CH + 1, 2 * CH) as i:
                for u in range(2):
                    body(i, u, *args)

        @block.sync
        def _(sp):
            sp.dma_start(dst_t.rearrange("r e -> (r e)")[0:E], dst).then_inc(s_pad, 16)
            sp.dma_start(X[:, 0:FULL, :], x[0:FULL * P, :].rearrange("(w p) f -> p w f", p=P)).then_inc(s_x, 16)
            sp.dma_start(src_t.rearrange("r e -> (r e)")[0:E], src).then_inc(s_pad, 16)
            sp.dma_start(ew_t.rearrange("r e -> (r e)")[0:E], ew).then_inc(s_pad, 16)
            sp.dma_start(ea_t.rearrange("r (e a) -> (r e) a", a=ED)[0:E, :], ea).then_inc(s_pad, 16)
            sp.wait_ge(s_const, 1)
            sp.dma_start(X[0:REST, FULL, :], x[FULL * P:N, :]).then_inc(s_x, 16)
            for part, value in fills:
                sp.dma_start(part, value).then_inc(s_pad, 16)
            sp.wait_ge(s_pad, PADS)
            linear = dst_all.rearrange("r e -> (r e)")
            for o, flat in ((dst_l, linear[0:PC * P]), (next_l, linear[1:PC * P + 1]),
                            (src_l, src_t.rearrange("r e -> (r e)")), (ew_l, ew_t.rearrange("r e -> (r e)"))):
                sp.dma_start(o, flat.rearrange("(p c) -> p c", p=P)).then_inc(s_lin, 16)
            sp.wait_ge(s_order, 1)
            sp.dma_start(tile_dst.bitcast(i32), dst_t.rearrange("(b p) e -> p b e", p=P)).then_inc(s_tdst, 16)
            sp.wait_ge(s_toff, 2)
            sp.dma_start(win_d.rearrange("(b p) a -> p b a", p=P), wofi[:, :].unsqueeze(2),
                         allow_slow_non_contiguous=True).then_inc(s_pw, 16)
            sp.wait_ge(s_loc, 1)
            sp.dma_start(loc_p.rearrange("(b p) e -> p b e", p=P), rows_locb).then_inc(s_pw, 16)
            sp.dma_start(src_p.rearrange("(b p) e -> p b e", p=P), rows_srcf).then_inc(s_pw, 16)
            sp.wait_ge(s_pw, 48)
            sp.dma_start(win[:, :], win_d.rearrange("r a -> a r")).then_inc(s_win, 16)
            for b in range(PB):
                sp.wait_ge(s_eag[b % 2], 16 * (b // 2 + 1))
                sp.dma_start(ea_p[b * P:(b + 1) * P, :], rows_ea[:, b % 2, :]).then_inc(s_eaw[b % 2], 16)
            sp.wait_ge(s_pta, 2 * ((PB + 3) // 4))
            sp.dma_start(ew_pc, ew_cols).then_inc(s_ewp, 16)
            sp.wait_ge(s_h, 1)
            sp.dma_start(table[0].rearrange("(w p) f -> p w f", p=P), H).then_inc(s_tab[0], 16)
            for k in range(TABLES):
                sp.dma_start(sums[k].rearrange("(w p) f -> p w f", p=P),
                             zeros[:, :].unsqueeze(1).broadcast_to([P, W + 1, F])).then_inc(s_zero, 16)
            sp.wait_ge(s_z, 1)
            sp.dma_start(winrow, win_d.rearrange("r a -> a r").broadcast_to([P, PC])).then_inc(s_wrow, 16)
            sp.wait_ge(s_h, 2)
            sp.dma_start(table[1].rearrange("(w p) f -> p w f", p=P), H).then_inc(s_tab[1], 16)
            sp.wait_ge(s_att, 1)
            for u in range(2):
                sp.wait_ge(s_eaw[u], 16 * len(range(u, PB, 2)))

            def load_attention(i, u):
                sp.wait_ge(s_mem, i + CH * u + CH)
                rows = loc_p[bass.ds(i + CH * u, CH), :].rearrange("(a j) e -> a (j e)", a=1)
                sp.dma_start(locrow[:, u, :], rows.broadcast_to([P, CH * P])).then_inc(s_lr[u], 2 * CH)
                sp.wait_ge(s_use, PC + i + CH * u + CH)
                sp.dma_start(G_att[u][:, :, F + 1:FX],
                             ea_p[bass.ds(i + CH * u, CH), :].rearrange("j (e a) -> e j a", a=ED)).then_inc(s_ea[u], 2 * CH)

            loop(sp, load_attention, PC)
            sp.wait_ge(s_acc, PC)
            sp.wait_ge(s_ewp, 16)
            sp.dma_start(aux_c[:, :], ew_pc).then_inc(s_aux, 16)
            sp.wait_ge(s_h, 3)

            def load_src_rows(i, u):
                sp.wait_ge(s_m2, i + CH * u + CH)
                rows = src_p[bass.ds(i + CH * u, CH), :].rearrange("(a j) e -> a (j e)", a=1)
                sp.dma_start(srcrow[:, u, :], rows.broadcast_to([P, CH * P])).then_inc(s_sr[u], 2 * CH)

            loop(sp, load_src_rows, PC)
            for k in range(TABLES):
                sp.wait_ge(s_sc[k], 16 * PC // TABLES)
            sp.wait_ge(s_y, 16 + PC)
            for b, (w0_, n) in enumerate(BLK):
                if b >= 2:
                    sp.wait_ge(s_tr, 4 * NB + b - 1)
                for k in range(TABLES):
                    sp.dma_start(blkbuf[:, b % 2, k, 0:n, :],
                                 sums[k][w0_ * P:(w0_ + n) * P, :].rearrange("(w p) f -> p w f", p=P)).then_inc(s_bl[b % 2], 16)
            sp.wait_ge(s_h, 4)
            sp.dma_start(table[2].rearrange("(w p) f -> p w f", p=P), H).then_inc(s_tab[2], 16)
            sp.wait_ge(s_moc, 5 * NB)
            sp.dma_start(out[0:FULL * P, :].rearrange("(w p) f -> p w f", p=P), X[:, 0:FULL, :]).then_inc(s_out, 16)
            sp.dma_start(out[FULL * P:N, :], X[0:REST, FULL, :]).then_inc(s_out, 16)
            sp.wait_ge(s_out, 32)

        @block.gpsimd
        def _(pool):
            pool.iota(iota_i[:, :], [[1, P]], base=0, channel_multiplier=0).then_inc(s_iota, 1)
            pool.iota(iota_p[:, :], [[0, 1]], base=0, channel_multiplier=1).then_inc(s_iota, 1)
            pool.wait_ge(s_lin, 64)
            pool.wait_ge(s_place, 1)
            with pool.If(load_flag(ENG.Pool) > 0):
                pool.dma_start(ea_p, ea_t).then_inc(s_copy, 16)
                pool.wait_ge(s_copy, 16)
                with pool.Fori(0, PC - CH + 1, CH) as c:
                    linear_attr = ea_p.rearrange("r (e a) -> (r e) a", a=ED).rearrange("(p c) a -> p c a", p=P)
                    pool.dma_start(attr_s, linear_attr[:, bass.ds(c, CH), :]).then_inc(s_stage, CH)
                    for o, a in ((place_s, place), (src_s, src_l), (dst_s, dst_l), (ew_s, ew_l)):
                        nc.gpsimd.tensor_copy(o, a[:, bass.ds(c, CH)]).then_inc(s_take, CH // 4)
                    pool.wait_ge(s_stage, c + CH)
                    pool.wait_ge(s_take, c + CH)
                    pool.sem_inc(s_taken, 1)
                    for j in range(CH):
                        at_place = bass.IndirectOffsetOnAxis(ap=place_s[:, j:j + 1], axis=0)
                        for t, a in ((dst_t.rearrange("r (e a) -> (r e) a", a=1), dst_s[:, j:j + 1]),
                                     (src_t.rearrange("r (e a) -> (r e) a", a=1), src_s[:, j:j + 1]),
                                     (ew_t.rearrange("r (e a) -> (r e) a", a=1), ew_s[:, j:j + 1]),
                                     (ea_t.rearrange("r (e a) -> (r e) a", a=ED), attr_s[:, j, :])):
                            pool.indirect_dma_start(out=t, out_offset=at_place, in_=a, in_offset=None).then_inc(s_put, 16)
                    pool.wait_ge(s_put, 64 * c + 64 * CH)
            pool.sem_inc(s_order, 1)
            pool.wait_ge(s_toff, 1)
            pool.sem_inc(s_claim, 1)
            for b in range(PB):
                tile = bass.IndirectOffsetOnAxis(ap=toff[:, b:b + 1], axis=0)
                for t, rows in ((dst_t, rows_dst.bitcast(i32)), (src_t, rows_src.bitcast(i32)), (ew_t, rows_ew)):
                    pool.indirect_dma_start(out=rows[:, b, :], out_offset=None, in_=t, in_offset=tile).then_inc(s_rows, 16)
            for b in range(PB):
                tile = bass.IndirectOffsetOnAxis(ap=toff[:, b:b + 1], axis=0)
                if b == 0:
                    pool.wait_ge(s_ln0, 1)
                if b >= 2:
                    pool.wait_ge(s_eaw[b % 2], 16 * (b // 2))
                pool.indirect_dma_start(out=rows_ea[:, b % 2, :], out_offset=None, in_=ea_t, in_offset=tile).then_inc(s_eag[b % 2], 16)

            def gather(i, u, rows, slots, base):
                if not isinstance(i, int):
                    for q in range(4):
                        pool.wait_ge(s_g[4 * u + q], 2 * base + 2 * i)
                pool.sem_inc(s_claim, 1)
                nc.gpsimd.tensor_copy(idx_f[:, u, :], idx_c[:, bass.ds(i + CH * u, CH)]).then_inc(s_idx, CH)
                for q in range(4):
                    pool.wait_ge(s_use, base + i + CH * u + 4 * q + 4)
                    if q == 0:
                        pool.wait_ge(s_idx, base + i + CH * u + CH)
                    pool.sem_inc(s_claim, 1)
                    for j in range(4 * q, 4 * q + 4):
                        edge = bass.IndirectOffsetOnAxis(ap=idx_f[:, u, j:j + 1], axis=0)
                        pool.indirect_dma_start(out=slots[u][:, j, 0:F], out_offset=None, in_=rows,
                                                in_offset=edge).then_inc(s_g[4 * u + q], 16)

            pool.wait_ge(s_ptd, (PB + 3) // 4)
            pool.wait_ge(s_tab[0], 16)
            for u in range(2):
                gather(0, u, table[0], G_plain, 0)
            loop(pool, gather, PC, table[0], G_plain, 0, first=2 * CH)
            pool.wait_ge(s_att, 1)
            pool.wait_ge(s_tab[1], 16)
            loop(pool, gather, PC, table[1], G_att, PC)

            def scatter(i, u):
                for j in range(CH):
                    if j == 0:
                        pool.wait_ge(s_ix2, i + CH * u + CH)
                    if j % 4 == 0:
                        pool.wait_ge(s_yc, i + CH * u + j + 4)
                    if u + j // TABLES > 0 or not isinstance(i, int):
                        pool.wait_ge(s_sc[j % TABLES], (i + CH * u) * (16 // TABLES) + 16 * (j // TABLES))
                    pool.sem_inc(s_clm2, 1)
                    node = bass.IndirectOffsetOnAxis(ap=idx_f[:, u, j:j + 1], axis=0)
                    pool.indirect_dma_start(out=sums[j % TABLES], out_offset=node, in_=ysc[:, u, j, :],
                                            in_offset=None, compute_op=ALU.add).then_inc(s_sc[j % TABLES], 16)

            pool.sem_inc(s_clm2, 32)
            pool.wait_ge(s_zero, 16 * TABLES)
            for u in range(2):
                scatter(0, u)
            loop(pool, scatter, PC, first=2 * CH)
            pool.wait_ge(s_tab[2], 16)
            loop(pool, gather, PC, table[2], G_plain, 2 * PC)

        @block.vector
        def _(v):
            steps = [0]

            def step(ins):
                steps[0] += 1
                ins.then_inc(s_d, 1)
                v.wait_ge(s_d, steps[0])

            def tt(o, a, b, op):
                return v.tensor_tensor(o, a, b, op)

            def ts(o, a, s1, s2, op0, op1=ALU.bypass):
                return v.tensor_scalar(o, a, s1, s2, op0, op1)

            def reduce(o, a, op=ALU.add):
                return v.tensor_reduce(out=o, in_=a, op=op, axis=AX.X)

            v.wait_ge(s_iota, 2)
            step(v.tensor_copy(iota[:, :], iota_i[:, :]))
            step(v.tensor_copy(row[:, :], iota_p[:, :]))
            step(v.memset(ones[:, :], 1.0))
            step(v.memset(ones_b[:, :], 1.0))
            step(v.memset(zeros[:, :], 0.0))
            step(v.memset(far[:, :], FAR))
            step(v.memset(att[:, :, :], 0.0))
            step(v.memset(X[:, FULL, :], 0.0))
            step(ts(ident[:, :], iota[:, :], row[:, 0:1], None, ALU.is_equal))
            step(v.tensor_copy(ident_b[:, :], ident[:, :]))
            step(ts(lower[:, :], iota[:, :], row[:, 0:1], None, ALU.is_lt))
            step(ts(thr, iota[:, 0:K1], 1.0, float(P), ALU.add, ALU.mult))
            step(ts(dump[:, :], row[:, :], float(NP), None, ALU.add))
            step(ts(pair, iota[:, 0:PB], float(P), row[:, 0:1], ALU.mult, ALU.add))
            v.sem_inc(s_const, 1)

            def layer_norm(l):
                mean, var, dev, inv = (lns[:, k, :] for k in range(4))
                step(reduce(mean, X[:, :, :]))
                step(ts(mean, mean, 1.0 / F, None, ALU.mult))
                step(tt(H, X[:, :, :], mean.unsqueeze(2).broadcast_to([P, W, F]), ALU.subtract))
                v.sem_inc(s_lnc, 1)
                v.wait_ge(s_lnq, l + 1)
                step(reduce(var, HT[:, 0:NP].rearrange("p (w f) -> p w f", f=F)))
                step(ts(var, var, 1.0 / F, LN_EPS, ALU.mult, ALU.add))
                v.sem_inc(s_lnv, 1)
                v.wait_ge(s_lns, l + 1)
                step(v.reciprocal(inv, dev))
                step(v.scalar_tensor_tensor(H, H, 0.0, inv.unsqueeze(2).broadcast_to([P, W, F]), ALU.max, ALU.mult))

            v.wait_ge(s_lin, 64)
            step(tt(mask, dst_l, next_l, ALU.is_gt))
            step(reduce(order, mask, ALU.max))
            v.sem_inc(s_cmp, 1)
            step(ts(upper, iota[:, :], row[:, 0:1], None, ALU.is_gt))
            step(v.memset(R2[:, P:P + 2 * W1], 0.0))
            v.wait_ge(s_cmps, 1)
            step(v.tensor_copy(unordered[:, :], psum[:, 7, 0:1]))

            def placing(base, k, m):
                n = [0]

                def do(ins):
                    n[0] += 1
                    ins.then_inc(s_vp, 1)
                    v.wait_ge(s_vp, base + k * m + n[0])

                return do

            with v.If(load_flag(ENG.DVE) > 0):
                do = placing(0, 0, 0)
                do(ts(next_l, dst_l, P.bit_length() - 1, None, ALU.logical_shift_right))
                do(v.tensor_copy(hi, next_l))
                do(ts(hi, hi, float(W), None, ALU.min))
                do(v.memset(number, 0.0))
                do(v.memset(total, 0.0))
                with v.Fori(0, W1, 1) as k:
                    do = placing(5, k, 6)
                    do(ts(mask, hi, number, None, ALU.is_equal))
                    do(reduce(count, mask))
                    do(v.tensor_copy(in_window[:, bass.ds(k, 1)], count))
                    do(v.tensor_copy(before_window[:, bass.ds(k, 1)], total))
                    do(tt(total, total, count, ALU.add))
                    do(ts(number, number, 1.0, None, ALU.add))
            v.sem_inc(s_cw, 1)
            v.wait_ge(s_cws, 1)
            with v.If(load_flag(ENG.DVE) > 0):
                do = placing(5 + 6 * W1, 0, 0)
                do(v.tensor_copy(starts, psum[:, 7, 0:W1]))
                do(v.memset(number, 0.0))
                do(v.memset(placef, 0.0))
                with v.Fori(0, W1, 1) as k:
                    do = placing(8 + 6 * W1, k, 7)
                    do(ts(mask, hi, number, None, ALU.is_equal))
                    do(v.tensor_tensor_scan(ranks, mask, mask, 0.0, ALU.add, ALU.bypass))
                    do(v.tensor_copy(start, starts[:, bass.ds(k, 1)]))
                    do(ts(start, start, -1.0, None, ALU.add))
                    do(v.scalar_tensor_tensor(ranks, ranks, start, mask, ALU.add, ALU.mult))
                    do(tt(placef, placef, ranks, ALU.add))
                    do(ts(number, number, 1.0, None, ALU.add))
                do = placing(8 + 13 * W1, 0, 0)
                do(v.tensor_copy(place, placef))
            v.sem_inc(s_place, 1)

            v.wait_ge(s_tdst, 16)
            step(v.tensor_copy(last, tile_dst.bitcast(i32)[:, :, P - 1]))
            step(tt(cmp_k, last.unsqueeze(1).broadcast_to([P, K1, PB]), thr.unsqueeze(2).broadcast_to([P, K1, PB]), ALU.is_lt))
            step(reduce(cnt_k, cmp_k))
            v.sem_inc(s_cntk, 1)
            v.wait_ge(s_aps, 1)
            step(v.scalar_tensor_tensor(bnd, iota[:, 0:K1], 1.0, psum[:, 7, 0:K1], ALU.add, ALU.add))
            step(tt(cmp_p, bnd.unsqueeze(1).broadcast_to([P, PB, K1]), pair.unsqueeze(2).broadcast_to([P, PB, K1]), ALU.is_le))
            step(reduce(wof, cmp_p))
            step(tt(toff[:, :], pair, wof, ALU.subtract))
            v.sem_inc(s_toff, 1)
            step(v.tensor_copy(wofi[:, :], wof))
            v.sem_inc(s_toff, 1)
            step(ts(negw, wof, -float(P), None, ALU.mult))
            v.wait_ge(s_x, 32)
            layer_norm(0)
            v.sem_inc(s_ln0, 1)
            v.wait_ge(s_rows, 16 * 3 * PB)
            step(tt(rows_loc, rows_dst.bitcast(i32), negw.unsqueeze(2).broadcast_to([P, PB, P]), ALU.add))
            step(v.tensor_copy(rows_locb, rows_loc))
            step(v.tensor_copy(rows_srcf, rows_src.bitcast(i32)))
            v.sem_inc(s_loc, 1)
            PG = (PB + 3) // 4
            for g in range(PG):
                n = min(4, PB - 4 * g)
                v.wait_ge(s_pt, PG + g + 1)
                v.tensor_copy(idx_c[:, 4 * g * P:(4 * g + n) * P], psum[:, (PG + g) % 8, 0:n * P]).then_inc(s_ptd, 1)

            v.wait_ge(s_pta, PG)

            def degree_one_hots(i, u):
                v.wait_ge(s_dm, i + CH * u + CH)
                tt(onehot_b[:, u], loc_c[:, bass.ds(i + CH * u, CH)].unsqueeze(2).broadcast_to([P, CH, P]),
                   iota[:, :].unsqueeze(1).broadcast_to([P, CH, P]), ALU.is_equal).then_inc(s_oh, CH)

            loop(v, degree_one_hots, PC)
            v.wait_ge(s_pt, 3 * PG)
            step(tt(selector, wof.unsqueeze(2).broadcast_to([P, PB, W]), iota[:, 0:W].unsqueeze(1).broadcast_to([P, PB, W]), ALU.is_equal))
            v.sem_inc(s_sel, 1)
            v.wait_ge(s_deg, 1)
            step(ts(dinv[:, :], psum[:, 4, 0:W], 1.0, None, ALU.add))
            v.sem_inc(s_dg, 1)
            v.wait_ge(s_dgr, 1)
            step(v.reciprocal(dinv[:, :], dinv[:, :]))

            dinv_b = dinv[:, :].unsqueeze(2).broadcast_to([P, W, F])
            step(tt(H, H, dinv_b, ALU.mult))
            v.sem_inc(s_h, 1)
            v.wait_ge(s_win, 16)

            def plain_sums(i, u, base, oh_base):
                v.wait_ge(s_use, base + i + CH * u + CH)
                tt(onehot[:, u], loc_c[:, bass.ds(i + CH * u, CH)].unsqueeze(2).broadcast_to([P, CH, P]),
                   iota[:, :].unsqueeze(1).broadcast_to([P, CH, P]), ALU.is_equal).then_inc(s_oh, CH)
                for q in range(4):
                    w = load_windows(ENG.DVE, i + CH * u + 4 * q, 4)
                    v.wait_ge(s_use, 32 + base + i + CH * u + 4 * q + 4)
                    for j in range(4 * q, 4 * q + 4):
                        v.wait_ge(s_add, 16 + oh_base + i + CH * u + j)
                        rows = ACC[:, bass.ds(w[j - 4 * q], 1), 0:F].rearrange("p a f -> p (a f)")
                        tt(rows, rows, bank4(j // 4)[:, j % 4, :], ALU.add).then_inc(s_add, 1)

            step(v.memset(accflat[:, 0:W * FX], 0.0))
            v.sem_inc(s_add, 16)
            v.wait_ge(s_add, 16)
            loop(v, plain_sums, PC, 0, 0)
            v.wait_ge(s_add, 16 + PC)
            step(tt(ACC[:, :, 0:F], ACC[:, :, 0:F], H, ALU.add))
            step(tt(ACC[:, :, 0:F], ACC[:, :, 0:F], dinv_b, ALU.mult))
            v.sem_inc(s_z, 1)

            def batch_norm(l, use, gamma):
                total, mean, sq, dev, inv = (bns[:, k:k + 1] for k in range(5))
                v.wait_ge(s_moc, (use + 1) * NB)
                step(reduce(total, HT[:, 0:N]))
                step(ts(mean, total, 1.0 / N, None, ALU.mult))
                step(ts(HT[:, 0:N], HT[:, 0:N], mean, None, ALU.subtract))
                v.sem_inc(s_bnc, 1)
                v.wait_ge(s_bnq, l + 1)
                step(ts(dev, sq, 1.0 / N, BN_EPS, ALU.mult, ALU.add))
                v.sem_inc(s_bnv, 1)
                v.wait_ge(s_bns, l + 1)
                step(v.reciprocal(inv, dev))
                step(tt(inv, inv, gamma, ALU.mult))
                v.sem_inc(s_bna, 1)
                for b, (w0_, n) in enumerate(BLK):
                    v.wait_ge(s_bt, l * NB + b + 1)
                    full = n if w0_ + n < W else n - 1
                    if full:
                        o = X[:, w0_:w0_ + full, :]
                        ins = tt(o, o, bank4(4 + b % 2)[:, 0:full, :], ALU.add)
                    if full < n:
                        o = X[0:REST, FULL, :]
                        ins = tt(o, o, bank4(4 + b % 2)[0:REST, full, :], ALU.add)
                    ins.then_inc(s_btc, 1)
                v.wait_ge(s_btc, (l + 1) * NB)

            batch_norm(0, 0, cols[:, 1:2])

            layer_norm(1)
            v.sem_inc(s_h, 1)
            v.wait_ge(s_wrow, 16)
            same_w = R2[:, PC // 2:PC // 2 + PC - 1]
            step(tt(same_w, winrow[:, 1:PC], winrow[:, 0:PC - 1], ALU.is_equal))
            v.wait_ge(s_ewp, 16)
            step(ts(aux_c[:, 1:PC], same_w, -2.0 * NOTHING, NOTHING, ALU.mult, ALU.add))
            step(v.memset(aux_c[:, 0:1], NOTHING))
            for q, (w0_, n) in enumerate(QB):
                v.wait_ge(s_qh, q + 1)
                high = Q3[:, 0, w0_:w0_ + n, :]
                rem = qrem[:, 3 * (q % 2):3 * (q % 2) + n, :]
                step(tt(rem, psum[:, 4 + q % 2, 0:n * FX].rearrange("p (w f) -> p w f", f=FX), high, ALU.subtract))
                v.sem_inc(s_qs, 1)
                step(v.tensor_copy(Q3[:, 1, w0_:w0_ + n, :], rem))
                step(tt(Q3[:, 2, w0_:w0_ + n, :], rem, Q3[:, 1, w0_:w0_ + n, :], ALU.subtract))
            step(v.memset(accflat[:, 0:W * FX], 0.0))
            v.wait_ge(s_tab[1], 16)
            v.wait_ge(s_trc, 2 * NB)
            for u in range(2):
                step(v.memset(G_att[u][:, :, F:F + 1], 1.0))
            step(tt(picks[:, :], ident[:, 0:GR], ident[:, GR:2 * GR], ALU.add))
            step(tt(picks[:, :], picks[:, :], ident[:, 2 * GR:3 * GR], ALU.add))
            step(v.tensor_copy(pick, picks[0:3 * GR, :].unsqueeze(2).broadcast_to([3 * GR, GR, P])))
            v.sem_inc(s_att, 1)
            v.sem_inc(s_mem, 32)
            score, oldm, newm, corr = (att[:, k, :] for k in range(4))

            windows = [None]

            def attention_vector(i, k):
                p = i + k
                if (k + 4) % CH == 0 and there(i, k + 4):
                    u = ((k + 4) // CH) % 2
                    v.wait_ge(s_lr[u], p + 4 - CH * u + 2 * CH)
                    if there(i, k - 13):
                        v.wait_ge(s_min, p - 12)
                    ts(member[:, u], pairs(locrow[:, u, :]), row[:, 0:1], None, ALU.is_equal)
                    ts(penalty[:, u], pairs(locrow[:, u, :]), row[:, 0:1], MASKED, ALU.not_equal, ALU.mult)
                    v.tensor_copy(col_f[:, u, 0, :], aux_c[:, bass.ds(p + 4, CH)]).then_inc(s_mem, CH)
                if there(i, k - 9):
                    a, u = (k - 9) % CH, ((k - 9) // CH) % 2
                    v.wait_ge(s_row, p - 8)
                    if there(i, k - 11):
                        v.wait_ge(s_exp, p - 10)
                    v.wait_ge(s_min, p - 9)
                    if a == 0:
                        v.wait_ge(s_mem, 32 + p - 9 + CH)
                    v.tensor_tensor(oldm[:, a:a + 1], newm[:, (a - 1) % CH:(a - 1) % CH + 1],
                                    col_f[:, u, 0, a:a + 1], ALU.max).then_inc(s_nmo, 1)
                if there(i, k - 12):
                    if k % 4 == 0:
                        windows[0] = load_windows(ENG.DVE, p - 12, 4)
                    a = (k - 12) % CH
                    v.wait_ge(s_use, PC + 32 + p - 12 + 1)
                    v.wait_ge(s_acc, p - 12)
                    if there(i, k - 9):
                        v.wait_ge(s_nmo, p - 8)
                    rows = ACC[:, bass.ds(windows[0][k % 4], 1), :].rearrange("p a f -> p (a f)")
                    v.scalar_tensor_tensor(rows, rows, corr[:, a:a + 1], psum[:, 6 + k % 2, 0:FX], ALU.mult,
                                           ALU.add).then_inc(s_acc, 1)
                g = (k // GR - 1) % 2
                if k % GR == 1 and there(i, k - 2):
                    v.wait_ge(s_shi, p - 1)
                    s = (k - 1 - GR) % CH
                    tt(rem_s[:, g, :], score[:, s:s + GR], parts[:, g, 0:GR], ALU.subtract).then_inc(s_srem, GR)
                if k % GR == 2 and there(i, k - 3):
                    v.wait_ge(s_smid, p - 2)
                    tt(parts[:, g, 2 * GR:3 * GR], rem_s[:, g, :], parts[:, g, GR:2 * GR], ALU.subtract).then_inc(s_slo, GR)
                if there(i, k - 9):
                    a, u = (k - 9) % CH, ((k - 9) // CH) % 2
                    if not there(i, k - 12):
                        v.wait_ge(s_nmo, p - 8)
                    v.tensor_tensor_reduce(out=masked[:, (k - 9) % 2, :], in0=psum[:, 2 + (k - 9) % 2, 0:P],
                                           in1=penalty[:, u, a, :], scale=1.0, scalar=oldm[:, a:a + 1],
                                           op0=ALU.add, op1=ALU.min, accum_out=newm[:, a:a + 1]).then_inc(s_min, 1)
                if there(i, k):
                    s = k % 32
                    if s % 4 == 0:
                        v.wait_ge(s_g[s // 4], 2 * PC + 2 * (p - s) + 64)
                    if s % CH == 0:
                        v.wait_ge(s_ea[s // CH], p - s + 32)
                    v.wait_ge(s_qe, p + 1)
                    v.tensor_tensor_reduce(out=junk[:, k % 2, :], in0=psum[:, k % 2, 0:FX],
                                           in1=G_att[s // CH][:, s % CH, :], scale=1.0, scalar=0.0, op0=ALU.mult,
                                           op1=ALU.add, accum_out=score[:, s % CH:s % CH + 1]).then_inc(s_dot, 1)

            attention(v, attention_vector)
            v.wait_ge(s_acc, PC)
            den = lns[:, 0, :]
            step(ts(den, ACC[:, :, F], 1.0e-37, None, ALU.max))
            step(v.reciprocal(den, den))
            step(tt(ACC, ACC, den.unsqueeze(2).broadcast_to([P, W, FX]), ALU.mult))
            v.sem_inc(s_agn, 1)
            batch_norm(1, 2, cols[:, 5:6])

            layer_norm(2)
            v.sem_inc(s_h, 1)
            v.sem_inc(s_m2, 32)
            v.wait_ge(s_aux, 16)
            v.sem_inc(s_small, CH)

            def combine_vector(i, u):
                p0 = i + CH * u
                idx = idx_c[:, bass.ds(p0, CH)]
                locf, ewf, idf = (col_f[:, u, k, :] for k in range(3))
                v.wait_ge(s_cm, p0 + CH)
                v.tensor_copy(locf, loc_c[:, bass.ds(p0, CH)])
                v.tensor_copy(ewf, aux_c[:, bass.ds(p0, CH)])
                v.tensor_copy(idf, idx).then_inc(s_col, CH)
                v.wait_ge(s_sr[u], i + 2 * CH)
                v.wait_ge(s_col, p0 + CH)
                tt(same[:, u], pairs(srcrow[:, u, :]), idf.unsqueeze(2).broadcast_to([P, CH, P]), ALU.is_equal).then_inc(s_same, CH)
                for j in range(CH):
                    v.tensor_scalar(onehot[:, u, j, :], iota[:, :], locf[:, j:j + 1], ewf[:, j:j + 1],
                                    ALU.is_equal, ALU.mult).then_inc(s_m2, 1)
                v.wait_ge(s_same, p0 + CH)
                v.wait_ge(s_small, CH + 4 * p0)
                tt(earlier, same[:, u], lower[:, :].unsqueeze(1).broadcast_to([P, CH, P]), ALU.mult).then_inc(s_ear, CH)
                v.wait_ge(s_ear, p0 + CH)
                reduce(dup, earlier).then_inc(s_small, CH)
                v.wait_ge(s_small, 4 * p0 + 2 * CH)
                ts(dup, dup, 1.0, None, ALU.min).then_inc(s_small, CH)
                ts(tgt, idf, -1.0, dump[:, 0:1], ALU.mult, ALU.add).then_inc(s_small, CH)
                v.wait_ge(s_small, 4 * p0 + 4 * CH)
                tt(tgt, tgt, dup, ALU.mult).then_inc(s_small, CH)
                v.wait_ge(s_small, 4 * p0 + 5 * CH)
                v.wait_ge(s_clm2, p0 + 24)
                tt(idx_f[:, u, :], tgt, idf, ALU.add).then_inc(s_ix2, CH)

            dup, tgt = att[:, 0, :], att[:, 1, :]
            loop(v, combine_vector, PC)

            def add_blocks(use):
                for b, (w0_, n) in enumerate(BLK):
                    v.wait_ge(s_mo, use * NB + b + 1)
                    o = X[:, w0_:w0_ + n, :]
                    tt(o, o, bank4(2 + b % 2)[:, 0:n, :], ALU.add).then_inc(s_moc, 1)
                v.wait_ge(s_moc, (use + 1) * NB)

            add_blocks(3)
            layer_norm(3)
            v.sem_inc(s_h, 1)
            step(v.memset(accflat[:, 0:W * FX], 0.0))
            loop(v, plain_sums, PC, 2 * PC, PC)
            v.wait_ge(s_add, 16 + 2 * PC)
            v.sem_inc(s_z, 1)
            add_blocks(4)

        @block.tensor
        def _(t):
            def mm(o, lhs_t, rhs, start=True, stop=True):
                return nc.tensor.matmul(o, lhs_t, rhs, start=start, stop=stop)

            t.wait_ge(s_w, WEIGHTS)
            t.wait_ge(s_const, 1)
            for k, m in enumerate((1, 2, 3, 4)):
                nc.tensor.transpose(bank4(6)[:, k, :], Wm[:, m, :], ident[:, :])
            nc.tensor.transpose(psum[0:X1, 5, 0:P], VX[:, :], ident[:, :]).then_inc(s_wt, 1)
            t.wait_ge(s_cmp, 1)
            mm(psum[:, 7, 0:1], ones[:, :], order).then_inc(s_cmps, 1)
            t.wait_ge(s_cw, 1)
            mm(psum[:, 7, 0:W1], upper, in_window, stop=False)
            mm(psum[:, 7, 0:W1], ones[:, :], before_window, start=False).then_inc(s_cws, 1)
            t.wait_ge(s_cntk, 1)
            mm(psum[:, 7, 0:K1], ones[:, :], cnt_k).then_inc(s_aps, 1)
            PG = (PB + 3) // 4
            t.wait_ge(s_loc, 1)
            t.wait_ge(s_wtc, 1)
            for a, rows in enumerate((rows_loc, rows_srcf, rows_ew)):
                for g in range(PG):
                    k = a * PG + g
                    n = min(4, PB - 4 * g)
                    if k >= 8:
                        b = k - 8
                        if b < PG:
                            t.wait_ge(s_pta, b + 1)
                        elif b < 2 * PG:
                            t.wait_ge(s_ptd, b - PG + 1)
                        else:
                            t.wait_ge(s_pta, b - PG + 1)
                    for j in range(n):
                        last_ins = nc.tensor.transpose(bank4(k % 8)[:, j, :], rows[:, 4 * g + j, :], ident[:, :])
                    last_ins.then_inc(s_pt, 1)
            t.sem_inc(s_dm, 32)
            t.wait_ge(s_pta, 2 * PG)
            t.wait_ge(s_ptd, PG)

            def count_degrees(i, u):
                t.wait_ge(s_oh, i + CH * u + CH)
                t.wait_ge(s_dmc, i + CH * u + CH)
                for j in range(CH):
                    mm(psum[:, u, j:j + 1], onehot_b[:, u, j, :], ones_b[:, :]).then_inc(s_dm, 1)

            loop(t, count_degrees, PC)
            t.wait_ge(s_dmc, 32 + PC)
            for g in range(PG):
                n = min(4, PB - 4 * g)
                for j in range(n):
                    b = 4 * g + j
                    last_ins = nc.tensor.transpose(bank4(g % 4)[:, j, :], counts[:, b * P:(b + 1) * P], ident[:, :])
                last_ins.then_inc(s_ct, 1)
            t.wait_ge(s_ctc, PG)
            t.wait_ge(s_sel, 1)
            for b in range(PB):
                last_ins = mm(psum[:, 4, 0:W], counts_t[:, b, :], selector[:, b, :], start=b == 0, stop=b == PB - 1)
            last_ins.then_inc(s_deg, 1)

            def plain_products(i, u, base, add_base):
                t.wait_ge(s_oh, PC + add_base + i + CH * u + CH)
                for q in range(4):
                    t.wait_ge(s_g[4 * u + q], 2 * base + 2 * i + 64)
                    t.wait_ge(s_add, add_base + i + CH * u + 4 * q + 4)
                    for j in range(4 * q, 4 * q + 4):
                        mm(bank4(j // 4)[:, j % 4, :], onehot[:, u, j, :], G_plain[u][:, j, 0:F]).then_inc(s_use, 1)

            def transposes(use, view, rows=P):
                t.wait_ge(s_trc, use * NB)
                for b, (w0_, n) in enumerate(BLK):
                    if b >= 2:
                        t.wait_ge(s_trc, use * NB + b - 1)
                    for j in range(n):
                        last_ins = nc.tensor.transpose(bank4(b % 2)[0:rows, j, :], view(w0_ + j), ident[:, :])
                    last_ins.then_inc(s_tr, 1)

            def products(use, emit):
                t.wait_ge(s_moc, use * NB)
                for b, (w0_, n) in enumerate(BLK):
                    if b >= 2:
                        t.wait_ge(s_moc, use * NB + b - 1)
                    emit(2 + b % 2, w0_, n).then_inc(s_mo, 1)

            def transposes_back(l):
                t.wait_ge(s_bn, l + 1)
                for b, (w0_, n) in enumerate(BLK):
                    if b >= 2:
                        t.wait_ge(s_btc, l * NB + b - 1)
                    for j in range(n):
                        w = w0_ + j
                        m = min(P, N - w * P)
                        last_ins = nc.tensor.transpose(bank4(4 + b % 2)[0:m, j, :], HT[:, w * P:w * P + m], ident[:, :])
                    last_ins.then_inc(s_bt, 1)

            t.sem_inc(s_use, 32)
            loop(t, plain_products, PC, 0, 0)
            t.wait_ge(s_z, 1)
            transposes(0, lambda w: ACC[:, w, 0:F])
            t.wait_ge(s_trc, NB)
            products(0, lambda bank, w, n: mm(psum[:, bank, 0:n * P], Wm[:, 0, :], HT[:, w * P:(w + n) * P]))
            transposes_back(0)
            t.wait_ge(s_h, 2)
            t.wait_ge(s_btc, NB)
            transposes(1, lambda w: H[:, w, :])
            t.wait_ge(s_trc, 2 * NB)
            products(1, lambda bank, w, n: mm(psum[:, bank, 0:n * P], WT[:, 0, :], HT[:, w * P:(w + n) * P]))
            t.wait_ge(s_moc, 2 * NB)
            for q, (w0_, n) in enumerate(QB):
                if q >= 2:
                    t.wait_ge(s_qs, q - 1)
                for j in range(n):
                    last_ins = mm(psum[:, 4 + q % 2, j * FX:(j + 1) * FX], QT[:, (w0_ + j) * P:(w0_ + j + 1) * P], C[:, :])
                last_ins.then_inc(s_q, 1)
            t.wait_ge(s_att, 1)
            score = att[:, 0, :]

            windows = [None]

            def attention_tensor(i, k):
                p = i + k
                if k % GR == 0 and there(i, k - 8):
                    t.wait_ge(s_stc, p - 4)
                if there(i, k - 10):
                    t.wait_ge(s_exp, p - 9)
                    if there(i, k - 12):
                        t.wait_ge(s_etc, p - 11)
                    nc.tensor.transpose(psum[:, 4 + k % 2, 0:P], Eb[:, k % 2, :], ident[:, :]).then_inc(s_et, 1)
                g = (k // GR) % 2
                if there(i, k - 8):
                    if there(i, k - 10):
                        t.wait_ge(s_min, p - 9)
                    mm(psum[:, 2 + k % 2, 0:P], pick[:, k % GR, :], ST[:, g, :]).then_inc(s_row, 1)
                if there(i, k + 1):
                    s = (k + 1) % 32
                    if s % 4 == 0 or k == LAST:
                        windows[0] = load_windows(ENG.PE, p + 1 - s % 4, 4)
                    if s % CH == 0:
                        t.wait_ge(s_mem, 32 + p + 1 + CH)
                    if there(i, k - 1):
                        t.wait_ge(s_dot, p)
                    for part in range(3):
                        ins = mm(psum[:, (k + 1) % 2, 0:FX], member[:, s // CH, s % CH, :],
                                 Q3[:, part, bass.ds(windows[0][s % 4], 1), :].rearrange("p a f -> p (a f)"),
                                 start=part == 0, stop=part == 2)
                    ins.then_inc(s_qe, 1)
                if k % GR == 3 and there(i, k - 4):
                    t.wait_ge(s_slo, p - 3)
                    if there(i, k - 11):
                        t.wait_ge(s_etc, p - 10)
                    nc.tensor.transpose(rows_ps, parts[:, 1 - g, :], ident_b[:, :]).then_inc(s_str, GR)
                if there(i, k - 11):
                    s = (k - 11) % 32
                    t.wait_ge(s_etc, p - 10)
                    if there(i, k - 13):
                        t.wait_ge(s_acc, p - 12)
                    mm(psum[:, 6 + (k - 11) % 2, 0:FX], ET[:, s % 4, :], G_att[s // CH][:, s % CH, :]).then_inc(s_use, 1)

            attention(t, attention_tensor)
            t.wait_ge(s_agn, 1)
            transposes(2, lambda w: ACC[:, w, 0:F])
            transposes(3, lambda w: ACC[:, w, F:FX], rows=X1)
            t.wait_ge(s_trc, 4 * NB)

            def attention_out(bank, w, n):
                nodes = slice(w * P, (w + n) * P)
                o = psum[:, bank, 0:n * P]
                mm(o, WT[:, 1, :], AGT[:, nodes], stop=False)
                mm(o, VXT[:, :], EXT[:, nodes], start=False, stop=False)
                return mm(o, WT[:, 2, :], HT[:, nodes], start=False)

            products(2, attention_out)
            transposes_back(1)
            t.wait_ge(s_h, 3)
            t.wait_ge(s_btc, 2 * NB)
            t.sem_inc(s_cm, 32)
            t.sem_inc(s_y, 16)

            def combine_tensor(i, u):
                p0 = i + CH * u
                for q in range(4):
                    w = load_windows(ENG.PE, p0 + 4 * q, 4)
                    t.wait_ge(s_m2, 32 + p0 + 4 * q + 4)
                    t.wait_ge(s_cmc, p0 + 4 * q + 4)
                    for j in range(4 * q, 4 * q + 4):
                        mm(bank4(q)[:, j % 4, :], onehot[:, u, j, :], same[:, u, j, :]).then_inc(s_cm, 1)
                    t.wait_ge(s_cmc, 16 + p0 + 4 * q + 4)
                    for j in range(4 * q, 4 * q + 4):
                        mm(bank4(4 + q)[:, j % 4, :], cmb[:, j, :],
                           H[:, bass.ds(w[j - 4 * q], 1), :].rearrange("p a f -> p (a f)")).then_inc(s_y, 1)

            loop(t, combine_tensor, PC)
            t.wait_ge(s_trc, 4 * NB)
            for b, (w0_, n) in enumerate(BLK):
                t.wait_ge(s_bl[b % 2], 16 * TABLES * (b // 2 + 1))
                if b >= 2:
                    t.wait_ge(s_trc, 4 * NB + b - 1)
                for j in range(n):
                    for k in range(TABLES):
                        last_ins = mm(bank4(b % 2)[:, j, :], blkbuf[:, b % 2, k, j, :], ident[:, :], start=k == 0, stop=k == TABLES - 1)
                last_ins.then_inc(s_tr, 1)
            t.wait_ge(s_trc, 5 * NB)

            def scattered_out(bank, w, n):
                for j in range(n):
                    o = bank4(bank)[:, j, :]
                    mm(o, HT[:, (w + j) * P:(w + j + 1) * P], WT[:, 3, :], stop=False)
                    ins = mm(o, ones[0:1, :], b2row[:, :], start=False)
                return ins

            products(3, scattered_out)
            loop(t, plain_products, PC, 2 * PC, PC)
            t.wait_ge(s_z, 2)
            transposes(5, lambda w: ACC[:, w, 0:F])
            transposes(6, lambda w: H[:, w, :])
            t.wait_ge(s_trc, 7 * NB)

            def plain_out(bank, w, n):
                for j in range(n):
                    o = bank4(bank)[:, j, :]
                    mm(o, HT[:, (w + j) * P:(w + j + 1) * P], Wm[:, 5, :], stop=False)
                    ins = mm(o, H3T[:, (w + j) * P:(w + j + 1) * P], Wm[:, 6, :], start=False)
                return ins

            products(4, plain_out)

        @block.scalar
        def _(act):
            def activation(o, a, f, **kw):
                return nc.scalar.activation(o, a, f, **kw)

            for k, m in enumerate((w0, wq, wv, wskip, w2, w3, wself)):
                act.dma_start(Wm[:, k, :], m).then_inc(s_w, 16)
            act.dma_start(C[:, 0:F], wk).then_inc(s_w, 16)
            for o, m in ((C[:, F:F + 1], bk), (VX[:, 0:1], bv), (cols[:, 0:1], b0), (cols[:, 1:2], g0),
                         (cols[:, 2:3], be0), (cols[:, 3:4], bq), (cols[:, 4:5], bskip), (cols[:, 5:6], g1),
                         (cols[:, 6:7], be1)):
                act.dma_start(o, m.rearrange("(p a) -> p a", a=1)).then_inc(s_w, 16)
            act.dma_start(C[:, F + 1:FX], we).then_inc(s_w, 16)
            act.dma_start(VX[:, 1:X1], we).then_inc(s_w, 16)
            act.dma_start(b2row[:, :], b2.rearrange("(a n) -> a n", a=1)).then_inc(s_w, 16)
            act.wait_ge(s_w, WEIGHTS)
            act.wait_ge(s_wt, 1)
            activation(cols[:, 7:8], cols[:, 3:4], ACT.Copy, scale=-SCALE)
            activation(VXT[:, :], psum[0:X1, 5, 0:P], ACT.Copy)
            activation(WT[:, :, :], bank4(6), ACT.Copy).then_inc(s_wtc, 1)

            def layer_norm(l):
                act.wait_ge(s_lnc, l + 1)
                activation(HT[:, 0:NP], hflat[:, 0:NP], ACT.Square).then_inc(s_lnq, 1)
                act.wait_ge(s_lnv, l + 1)
                activation(lns[:, 2, :], lns[:, 1, :], ACT.Sqrt).then_inc(s_lns, 1)

            layer_norm(0)
            PG = (PB + 3) // 4
            for a, o in ((0, loc_c[:, :]), (2, ew_cols)):
                for g in range(PG):
                    n = min(4, PB - 4 * g)
                    act.wait_ge(s_pt, a * PG + g + 1)
                    activation(o[:, 4 * g * P:(4 * g + n) * P], psum[:, (a * PG + g) % 8, 0:n * P], ACT.Copy).then_inc(s_pta, 1)
            act.sem_inc(s_dmc, 32)

            def copy_counts(i, u):
                act.wait_ge(s_dm, 32 + i + CH * u + CH)
                activation(counts[:, bass.ds(i + CH * u, CH)], psum[:, u, 0:CH], ACT.Copy).then_inc(s_dmc, CH)

            act.wait_ge(s_loc, 1)
            loop(act, copy_counts, PC)
            for g in range(PG):
                n = min(4, PB - 4 * g)
                act.wait_ge(s_ct, g + 1)
                activation(counts_t[:, 4 * g:4 * g + n, :], bank4(g % 4)[:, 0:n, :], ACT.Copy).then_inc(s_ctc, 1)
            act.wait_ge(s_dg, 1)
            activation(dinv[:, :], dinv[:, :], ACT.Sqrt).then_inc(s_dgr, 1)

            def copy_blocks(use, o, rows=P):
                for b, (w0_, n) in enumerate(BLK):
                    act.wait_ge(s_tr, use * NB + b + 1)
                    activation(o[:, w0_ * P:(w0_ + n) * P], psum[0:rows, b % 2, 0:n * P], ACT.Copy).then_inc(s_trc, 1)

            def use_products(use, o, func, bias, scale=1.0):
                for b, (w0_, n) in enumerate(BLK):
                    act.wait_ge(s_mo, use * NB + b + 1)
                    activation(o[:, w0_ * P:(w0_ + n) * P], psum[:, 2 + b % 2, 0:n * P], func, bias=bias, scale=scale).then_inc(s_moc, 1)

            def batch_norm(l, func, beta, scratch):
                act.wait_ge(s_bnc, l + 1)
                activation(scratch[:, 0:N], HT[:, 0:N], ACT.Square, accum_out=bns[:, 2:3]).then_inc(s_bnq, 1)
                act.wait_ge(s_bnv, l + 1)
                activation(bns[:, 3:4], bns[:, 3:4], ACT.Sqrt).then_inc(s_bns, 1)
                act.wait_ge(s_bna, l + 1)
                activation(HT[:, 0:N], HT[:, 0:N], func, bias=beta, scale=bns[:, 4:5]).then_inc(s_bn, 1)

            copy_blocks(0, HT)
            use_products(0, HT, ACT.Identity, cols[:, 0:1])
            batch_norm(0, ACT.Relu, cols[:, 2:3], hflat)
            layer_norm(1)
            copy_blocks(1, HT)
            use_products(1, QT, ACT.Identity, cols[:, 7:8], -SCALE)
            for q, (w0_, n) in enumerate(QB):
                act.wait_ge(s_q, q + 1)
                activation(Q3[:, 0, w0_:w0_ + n, :], psum[:, 4 + q % 2, 0:n * FX].rearrange("p (w f) -> p w f", f=FX),
                           ACT.Copy).then_inc(s_qh, 1)
            act.wait_ge(s_att, 1)
            score, oldm, newm, corr = (att[:, k, :] for k in range(4))

            def attention_scalar(i, k):
                p = i + k
                g = (k // GR - 1) % 2
                if k % GR == 0 and there(i, k - 1):
                    s = (k - GR) % CH
                    act.wait_ge(s_dot, p)
                    if there(i, k - 9):
                        act.wait_ge(s_str, p - 8)
                    activation(parts[:, g, 0:GR], score[:, s:s + GR], ACT.Copy).then_inc(s_shi, GR)
                if k % GR == 1 and there(i, k - 2):
                    act.wait_ge(s_srem, p - 1)
                    activation(parts[:, g, GR:2 * GR], rem_s[:, g, :], ACT.Copy).then_inc(s_smid, GR)
                if there(i, k - 9):
                    a = (k - 9) % CH
                    act.wait_ge(s_min, p - 8)
                    if there(i, k - 11):
                        act.wait_ge(s_et, p - 10)
                    activation(Eb[:, (k - 9) % 2, :], masked[:, (k - 9) % 2, :], ACT.Exp,
                               bias=newm[:, a:a + 1], scale=-1.0).then_inc(s_exp, 1)
                    activation(corr[:, a:a + 1], oldm[:, a:a + 1], ACT.Exp, bias=newm[:, a:a + 1],
                               scale=-1.0).then_inc(s_c, 1)
                if k % GR == 3 and there(i, k - 4):
                    act.wait_ge(s_str, p - 3)
                    if there(i, k - 12):
                        act.wait_ge(s_row, p - 11)
                    activation(ST[:, 1 - (k // GR) % 2, :], rows_ps, ACT.Copy).then_inc(s_stc, GR)

                if there(i, k - 10):
                    act.wait_ge(s_et, p - 9)
                    if there(i, k - 14):
                        act.wait_ge(s_use, PC + 32 + p - 13)
                    activation(ET[:, (k - 10) % 4, :], psum[:, 4 + k % 2, 0:P], ACT.Copy).then_inc(s_etc, 1)
            attention(act, attention_scalar)
            act.wait_ge(s_agn, 1)
            copy_blocks(2, AGT)
            copy_blocks(3, EXT, rows=X1)
            use_products(2, HT, ACT.Relu, cols[:, 4:5])
            batch_norm(1, ACT.Identity, cols[:, 6:7], AGT)
            layer_norm(2)
            act.wait_ge(s_h, 3)
            act.sem_inc(s_cmc, 16)

            def combine_scalar(i, u):
                p0 = i + CH * u
                for q in range(4):
                    act.wait_ge(s_cm, 32 + p0 + 4 * q + 4)
                    act.wait_ge(s_y, p0 + 4 * q + 4)
                    activation(cmb[:, 4 * q:4 * q + 4, :], bank4(q), ACT.Copy).then_inc(s_cmc, 4)
                    act.wait_ge(s_y, 16 + p0 + 4 * q + 4)
                    act.wait_ge(s_clm2, p0 + 4 * q + 12)
                    activation(ysc[:, u, 4 * q:4 * q + 4, :], bank4(4 + q), ACT.Copy).then_inc(s_yc, 4)

            loop(act, combine_scalar, PC)
            copy_blocks(4, HT)
            layer_norm(3)
            copy_blocks(5, HT)
            copy_blocks(6, H3T)


_INS = ["x", "src", "dst", "edge_attr_10", "edge_weight", "L0_gnn_weight", "L0_gnn_bias", "L0_gnn_gamma",
        "L0_gnn_beta", "L1_gnn_Wq", "L1_gnn_bq", "L1_gnn_Wk", "L1_gnn_bk", "L1_gnn_Wv", "L1_gnn_bv",
        "L1_gnn_We", "L1_gnn_Wskip", "L1_gnn_bskip", "L1_gnn_gamma", "L1_gnn_beta", "L2_gnn_W",
        "L2_gnn_b", "L3_gnn_W", "L3_gnn_W_self"]


def kernel(**inputs):
    import numpy as _np
    import concourse.bacc as _bacc
    from concourse import mybir as _mybir
    from concourse.bass_utils import run_bass_kernel_spmd as _run

    nc = _bacc.Bacc("TRN2", target_bir_lowering=False, num_devices=1)
    arrays, args = {}, []
    for name in _INS:
        a = _np.ascontiguousarray(inputs[name])
        arrays[f"in_{name}_dram"] = a
        args.append(nc.dram_tensor(f"in_{name}_dram", a.shape, _mybir.dt.from_np(a.dtype), kind="ExternalInput").ap())
    shape = inputs["x"].shape
    args.append(nc.dram_tensor("out_0_dram", shape, _mybir.dt.float32, kind="ExternalOutput").ap())
    gnn_kernel(nc, *args)
    r = _run(nc, [arrays], core_ids=[0])
    return r.results[0]["out_0_dram"]
```

```python
from contextlib import ExitStack

import concourse.bass as bass
from concourse import mybir

f32, bf16, i32, i16 = mybir.dt.float32, mybir.dt.bfloat16, mybir.dt.int32, mybir.dt.int16
ALU = mybir.AluOpType
ACT = mybir.ActivationFunctionType
AX = mybir.AxisListType
ENG = mybir.EngineType

P = 128
CH = 16
GR = 4
TABLES = 8
MASKED = 1.0e30
NOTHING = 1.0e29
LN_EPS = BN_EPS = 1e-5


def gnn_kernel(nc, x, src, dst, ea, ew, w0, b0, g0, be0, wq, bq, wk, bk, wv, bv, we, wskip, bskip,
               g1, be1, w2, b2, w3, wself, out):
    N, F = x.shape
    E = src.shape[0]
    ED = ea.shape[1]
    assert F == P
    W = (N + P - 1) // P
    NP = W * P
    T = (E + P - 1) // P
    PB = (T + W - 1 + P - 1) // P
    PC = PB * P
    NCH = PC // CH
    assert NCH % 2 == 0
    X1 = 1 + ED
    FX = F + X1
    SCALE = float(F) ** -0.5
    FAR = 1 << 13
    assert FAR >= NP + P
    FULL = N // P
    REST = N - FULL * P
    BLK = [(b, min(4, W - b)) for b in range(0, W, 4)]
    NB = len(BLK)
    QB = [(b, min(3, W - b)) for b in range(0, W, 3)]
    NQ = len(QB)

    def dram(name, shape, dt):
        return nc.dram_tensor(name, shape, dt).ap()

    W1 = W + 1
    ROWS = P * W1

    def by_partition(t):
        return t.rearrange("(p w) f -> p w f", p=P)

    src_t, dst_all = dram("src_tiles", [PC, P], i32), dram("dst_tiles", [PC + 1, P], i32)
    dst_t = dst_all[0:PC, :]
    ew_t, ea_t = dram("weight_tiles", [PC, P], f32), dram("attr_tiles", [PC, P * ED], f32)
    ea_p = dram("attr_pairs", [PC, P * ED], f32)
    src_p = dram("src_pairs", [PC, P], f32)
    loc_p = dram("local_dst_pairs", [PC, P], bf16)
    win_d = dram("window_of_pair", [PC, 1], i16)
    ew_pc = dram("weight_columns", [P, PC], f32)
    table = [dram(f"gather_table{l}", [ROWS, F], f32) for l in range(3)]
    sums = [dram(f"scattered_sums{k}", [ROWS, F], f32) for k in range(TABLES)]

    ctx = ExitStack()
    with ctx:
        def sb(name, shape, dt=f32):
            return ctx.enter_context(nc.sbuf_tensor(name, shape, dt))

        def sem(name):
            return ctx.enter_context(nc.semaphore(name))

        X = sb("X", [P, W, F])
        NH = max(W * F, CH * FX + CH * P + 13 * P + GR * P // 2)
        NR1 = max((3 * W * FX + 1) // 2, 5 * CH * P, max(4 * PC, CH * FX) + PC + PB * W, 2 * TABLES * 4 * P)
        hflat = sb("H", [P, NH])[:, :]
        H = hflat[:, 0:W * F].rearrange("p (w f) -> p w f", f=F)
        HT = sb("HT", [P, max(NP, 2 * P * ED + PC, 2 * PC, 3 * CH * P)])[:, :]
        accflat = sb("ACC", [P, max(W * FX, 2 * PC)])[:, :]
        ACC = accflat[:, 0:W * FX].rearrange("p (w f) -> p w f", f=FX)
        r1 = sb("R1", [P, NR1])[:, :]
        R2 = sb("R2", [P, 2 * CH * P], f32)
        G = sb("G", [P, CH, FX])
        loc_c = sb("loc_c", [P, PC])
        idx_c = sb("idx_c", [P, PC], i32)
        win = sb("win", [1, PC], i16)
        idx_f = sb("idx_f", [P, 2, CH], i32)
        col_f = sb("col_f", [P, 2, 3, CH])
        aux_c = sb("aux_c", [P, PC])
        att = sb("att", [P, 5, CH])
        iota_i = sb("iota_i", [P, P], i32)
        iota_p = sb("iota_p", [P, 1], i32)
        iota = sb("iota", [P, P])
        row = sb("row", [P, 1])
        ident = sb("ident", [P, P])
        ident_b = sb("ident_b", [P, P], bf16)
        ones = sb("ones", [P, P])
        ones_b = sb("ones_b", [P, 1], bf16)
        zeros = sb("zeros", [P, P])
        far = sb("far", [P, P], i32)
        dinv = sb("dinv", [P, W])
        lns = sb("lns", [P, 4, W])
        bns = sb("bns", [P, 8])
        cols = sb("cols", [P, 8])
        b2row = sb("b2row", [1, F])
        Wm = sb("Wm", [P, 7, P])
        WT = sb("WT", [P, 4, P])
        C = sb("C", [P, FX])
        VX = sb("VX", [P, X1])
        VXT = sb("VXT", [X1, P])

        r2b = R2[:, :].bitcast(bf16)

        def pairs(ap):
            return ap.rearrange("p (b e) -> p b e", e=P)

        rows_src, rows_dst, rows_ew = (pairs(r1[:, k * PC:(k + 1) * PC]) for k in range(3))
        rows_locb = pairs(r1[:, 3 * PC:3 * PC + PC // 2].bitcast(bf16))
        tile_dst = pairs(accflat[:, 0:PC])
        rows_loc = pairs(accflat[:, PC:2 * PC])
        rows_ea = HT[:, 0:2 * P * ED].rearrange("p (u a) -> p u a", u=2)
        at = max(4 * PC, CH * FX)
        ew_cols = r1[:, at:at + PC]
        selector = r1[:, at + PC:at + PC + PB * W].rearrange("p (b w) -> p b w", w=W)
        rows_srcf = pairs(HT[:, 2 * P * ED:2 * P * ED + PC])
        prep = sb("prep", [P, 4 * PB + 3 * (W - 1)])
        last, pair, wof, negw = (prep[:, i * PB:(i + 1) * PB] for i in range(4))
        K1 = W - 1
        thr, cnt_k, bnd = (prep[:, 4 * PB + i * K1:4 * PB + (i + 1) * K1] for i in range(3))
        toff = sb("toff", [P, PB], i32)
        wofi = sb("wofi", [P, PB], i16)
        dst_l, next_l, place = (r1[:, k * PC:(k + 1) * PC].bitcast(i32) for k in range(3))
        hi, mask = (r1[:, k * PC:(k + 1) * PC] for k in range(3, 5))
        src_l, ew_l = accflat[:, 0:PC].bitcast(i32), accflat[:, PC:2 * PC]
        placef, ranks = HT[:, 0:PC], HT[:, PC:2 * PC]
        upper = R2[:, 0:P]
        in_window, before_window, starts = (R2[:, P + k * W1:P + (k + 1) * W1] for k in range(3))
        number, count, total, start, order = (R2[:, P + 3 * W1 + k:P + 3 * W1 + k + 1] for k in range(5))
        at = P + 3 * W1 + 5
        attr_s = R2[:, at:at + CH * ED].rearrange("p (c a) -> p c a", a=ED)
        at += CH * ED
        place_s, src_s, dst_s = (R2[:, at + k * CH:at + (k + 1) * CH].bitcast(i32) for k in range(3))
        ew_s = R2[:, at + 3 * CH:at + 4 * CH]
        cmp_k = R2[:, 0:K1 * PB].rearrange("p (k b) -> p k b", b=PB)
        cmp_p = R2[:, 0:K1 * PB].rearrange("p (b k) -> p b k", k=K1)
        counts = accflat[:, 0:PC]
        counts_t = pairs(accflat[:, PC:2 * PC])
        onehot = R2[:, :].rearrange("p (u j n) -> p u j n", u=2, j=CH)
        onehot_b = r2b[:, 0:2 * CH * P].rearrange("p (u j n) -> p u j n", u=2, j=CH)
        G_plain = [G[:, :, :], r1[:, 0:CH * FX].rearrange("p (j f) -> p j f", f=FX)]
        Q3 = r1.bitcast(bf16)[:, 0:3 * W * FX].rearrange("p (t w f) -> p t w f", t=3, w=W)
        QT = accflat[:, 0:NP]
        member = r2b[:, 0:2 * CH * P].rearrange("p (u j e) -> p u j e", u=2, j=CH)
        penalty = r2b[:, 2 * CH * P:4 * CH * P].rearrange("p (u j e) -> p u j e", u=2, j=CH)
        G_att = [G[:, :, :], hflat[:, 0:CH * FX].rearrange("p (j f) -> p j f", f=FX)]
        at = CH * FX
        locrow = hflat[:, at:at + CH * P].bitcast(bf16).rearrange("p (u m) -> p u m", u=2)
        at += CH * P
        masked = hflat[:, at:at + 8 * P].rearrange("p (j e) -> p j e", e=P)
        at += 8 * P
        ET = hflat[:, at:at + 4 * P].rearrange("p (j n) -> p j n", n=P)
        at += 4 * P
        ST = hflat[:, at:at + P].bitcast(bf16)[0:3 * GR, :].rearrange("r (g e) -> r g e", g=2)
        at += P
        pick = hflat[:, at:at + GR * P // 2].bitcast(bf16)[0:3 * GR, :].rearrange("r (j n) -> r j n", j=GR)
        at += GR * P // 2
        assert at <= NH
        winrow = R2[:, 0:PC // 2].bitcast(i16)
        qrem = R2[:, 0:6 * FX].rearrange("p (i f) -> p i f", f=FX)
        EXT = r1[0:X1, 0:NP]
        srcrow = r1[:, 0:2 * CH * P].rearrange("p (u m) -> p u m", u=2)
        same = r1[:, 2 * CH * P:4 * CH * P].rearrange("p (u j e) -> p u j e", u=2, j=CH)
        cmb = r1[:, 4 * CH * P:5 * CH * P].rearrange("p (j e) -> p j e", e=P)
        ysc = HT[:, 0:2 * CH * P].rearrange("p (u j f) -> p u j f", u=2, j=CH)
        earlier = HT[:, 2 * CH * P:3 * CH * P].rearrange("p (j e) -> p j e", e=P)
        blkbuf = r1[:, 0:2 * TABLES * 4 * P].rearrange("p (u k w f) -> p u k w f", u=2, k=TABLES, w=4)
        H3T = r1[:, 0:NP]
        AGT = hflat[:, 0:NP]
        unordered = sb("unordered", [P, 1], i32)
        dump = sb("dump", [P, 1])
        junk = sb("junk", [P, 2, FX])
        parts = sb("parts", [P, 2, 3 * GR], bf16)
        rem_s = sb("rem_s", [P, 2, GR])
        picks = sb("picks", [P, GR])
        lower = sb("lower", [P, P])

        psum = ctx.enter_context(nc.psum_tensor("psum", [P, 8, 512], f32))

        rows_ps = psum[0:3 * GR, 5, 2 * P:2 * P + P // 2].bitcast(bf16)

        def bank4(b):
            return psum[:, b, :].rearrange("p (k f) -> p k f", f=P)

        s_w = sem("weights_loaded")
        s_wt = sem("weights_transposed")
        s_wtc = sem("transposed_weights_copied")
        s_x = sem("x_loaded")
        s_iota = sem("iota_written")
        s_const = sem("constants_written")
        s_padd = sem("dst_table_filled")
        s_pad = sem("src_and_weight_tables_filled")
        s_pade = sem("attribute_table_filled")
        s_linb = sem("linear_src_and_weights_loaded")
        s_lin = sem("linear_edges_loaded")
        s_cmp = sem("orders_compared")
        s_cmps = sem("orders_summed")
        s_flag = sem("order_known")
        s_cw = sem("edges_of_windows_counted")
        s_cws = sem("starts_of_windows_summed")
        s_place = sem("places_known")
        s_vp = sem("placing_step")
        s_copy = sem("attributes_set_aside")
        s_stage = sem("records_loaded")
        s_take = sem("records_copied")
        s_taken = sem("records_claimed")
        s_put = sem("records_placed")
        s_order = sem("edge_tables_in_order")
        s_tdst = sem("tile_dst_loaded")
        s_cntk = sem("boundaries_counted")
        s_aps = sem("boundaries_summed")
        s_toff = sem("tile_of_pair_known")
        s_drow = sem("pair_rows_of_dst_gathered")
        s_rows = sem("pair_rows_gathered")
        s_srcf = sem("src_rows_are_numbers")
        s_eag = [sem("attr_rows_gathered0"), sem("attr_rows_gathered1")]
        s_eaw = [sem("attr_rows_stored0"), sem("attr_rows_stored1")]
        s_loc = sem("pair_rows_are_numbers")
        s_pw = sem("pair_rows_stored")
        s_win = sem("window_row_loaded")
        s_pt = sem("pair_rows_transposed")
        s_pta = sem("pair_columns_copied_by_scalar")
        s_ptd = sem("pair_columns_copied_by_vector")
        s_ewp = sem("weight_columns_stored")
        s_d = sem("vector_step")
        s_oh = sem("one_hots_written")
        s_dm = sem("pair_counted")
        s_dmc = sem("pair_count_copied")
        s_ct = sem("counts_transposed")
        s_ctc = sem("transposed_counts_copied")
        s_sel = sem("selectors_written")
        s_deg = sem("degrees_summed")
        s_dg = sem("degrees_in_sbuf")
        s_dgr = sem("degree_roots")
        s_ln0 = sem("first_norm_done")
        s_lnc = sem("rows_centred")
        s_lnq = sem("rows_squared")
        s_lnv = sem("row_variances")
        s_lns = sem("row_deviations")
        s_h = sem("h_ready")
        s_tab = [sem(f"gather_table{l}_stored") for l in range(3)]
        s_zero = sem("scattered_sums_zeroed")
        s_g = [sem(f"rows_gathered{k}") for k in range(8)]
        s_idx = sem("indices_placed")
        s_claim = sem("group_claimed")
        s_use = sem("rows_used")
        s_add = sem("pair_added")
        s_z = sem("sums_ready")
        s_tr = sem("block_transposed")
        s_trc = sem("block_copied")
        s_mo = sem("block_product")
        s_moc = sem("block_product_used")
        s_bnc = sem("columns_centred")
        s_bnq = sem("columns_squared")
        s_bnv = sem("column_variance")
        s_bns = sem("column_deviation")
        s_bna = sem("column_scale")
        s_bn = sem("columns_normalised")
        s_bt = sem("block_transposed_back")
        s_btc = sem("block_added_to_x")
        s_wrow = sem("window_rows_loaded")
        s_aux = sem("weight_columns_loaded")
        s_q = sem("queries_product")
        s_qh = sem("queries_high_part")
        s_qs = sem("queries_split")
        s_att = sem("attention_ready")
        s_lr = [sem("local_rows_loaded0"), sem("local_rows_loaded1")]
        s_ea = [sem(f"attrs_loaded{k}") for k in range(4)]
        s_mem = sem("members_written")
        s_qe = sem("queries_spread")
        s_dot = sem("score_ready")
        s_shi = sem("scores_high_part")
        s_srem = sem("scores_remainder")
        s_smid = sem("scores_middle_part")
        s_slo = sem("scores_low_part")
        s_str = sem("score_parts_transposed")
        s_stc = sem("score_rows_copied")
        s_row = sem("scores_as_row")
        s_vclaim = sem("minimum_claimed")
        s_nmo = sem("old_maximum_ready")
        s_min = sem("new_maximum_ready")
        s_exp = sem("exponentials_ready")
        s_c = sem("correction_ready")
        s_et = sem("exponentials_transposed")
        s_etc = sem("exponentials_copied")
        s_acc = sem("attention_added")
        s_agn = sem("attention_normalised")
        s_sr = [sem("src_rows_loaded0"), sem("src_rows_loaded1")]
        s_m2 = sem("same_and_weighted_written")
        s_col = sem("columns_placed")
        s_same = sem("equal_src_written")
        s_ear = sem("earlier_edges_written")
        s_small = sem("duplicates_step")
        s_cm = sem("combination_ready")
        s_cmc = sem("combination_copied")
        s_y = sem("rows_to_scatter_ready")
        s_yc = sem("rows_to_scatter_copied")
        s_ix2 = sem("scatter_indices_ready")
        s_clm2 = sem("scatter_claimed")
        s_sc = [sem(f"scattered{k}") for k in range(TABLES)]
        s_bl = [sem("sum_blocks_loaded0"), sem("sum_blocks_loaded1")]
        s_out = sem("output_stored")

        block = ctx.enter_context(nc.Block())

        TAIL = T * P - E
        assert 0 < TAIL and 0 < REST

        def fills(t, fill, m, end):
            for r0, r1_, c0 in [(T - 1, T, (P - TAIL) * m)] + [(r, min(r + P, end), 0) for r in range(T, end, P)]:
                for c in range(c0, P * m, P):
                    n = min(P, P * m - c)
                    yield t[r0:r1_, c:c + n], fill[0:r1_ - r0, 0:n]

        dst_fills = list(fills(dst_all, far[:, :], 1, PC + 1))
        src_ew_fills = list(fills(src_t, zeros[:, :].bitcast(i32), 1, PC)) + list(fills(ew_t, zeros[:, :], 1, PC))
        attr_fills = list(fills(ea_t, zeros[:, :], ED, PC))
        WEIGHTS = 16 * (7 + 1 + 9 + 3)
        DST_PADS, PADS, ATTR_PADS = 16 * (1 + len(dst_fills)), 16 * (2 + len(src_ew_fills)), 16 * (1 + len(attr_fills))

        def load_windows(eng, first, n):
            return nc.values_load_multi_w_load_instructions(
                win[0:1, bass.ds(first, n)], engines=[eng], min_val=0, max_val=W - 1,
                skip_runtime_bounds_check_because="a count of at most W - 1 boundaries")[1]

        def load_flag(eng):
            return nc.values_load_multi_w_load_instructions(
                unordered[0:1, 0:1], engines=[eng], min_val=0, max_val=P,
                skip_runtime_bounds_check_because="a count of partitions")[1][0]

        LAST = 20
        TURNS = (PC - 54) // 32 + 1
        assert PC >= 64

        def there(i, k):
            return not isinstance(i, int) or 0 <= i + k < PC

        def peeled(i):
            return isinstance(i, int)

        def attention(eng, body):
            for k in range(-4, LAST, 2):
                body(0, k)
            with eng.Fori(0, 32 * (TURNS - 1) + 1, 32) as i:
                for k in range(LAST, LAST + 32, 2):
                    body(i, k)
            for k in range(LAST, PC + LAST - 32 * TURNS, 2):
                body(32 * TURNS, k)

        def two(bank, k, width):
            return psum[:, bank + k // 2 % 2, k % 2 * width:(k % 2 + 1) * width]

        def loop(eng, body, n, *args, first=0):
            with eng.Fori(first, n - 2 * CH + 1, 2 * CH) as i:
                for u in range(2):
                    body(i, u, *args)

        @block.sync
        def _(sp):
            sp.dma_start(dst_t.rearrange("r e -> (r e)")[0:E], dst).then_inc(s_padd, 16)
            sp.wait_ge(s_const, 1)
            for part, value in dst_fills:
                sp.dma_start(part, value).then_inc(s_padd, 16)
            sp.wait_ge(s_padd, DST_PADS)
            linear = dst_all.rearrange("r e -> (r e)")
            for o, flat in ((dst_l, linear[0:PC * P]), (next_l, linear[1:PC * P + 1])):
                sp.dma_start(o, flat.rearrange("(p c) -> p c", p=P)).then_inc(s_lin, 16)
            sp.dma_start(X[:, 0:FULL, :], x[0:FULL * P, :].rearrange("(w p) f -> p w f", p=P)).then_inc(s_x, 16)
            sp.dma_start(X[0:REST, FULL, :], x[FULL * P:N, :]).then_inc(s_x, 16)
            sp.dma_start(src_t.rearrange("r e -> (r e)")[0:E], src).then_inc(s_pad, 16)
            sp.dma_start(ew_t.rearrange("r e -> (r e)")[0:E], ew).then_inc(s_pad, 16)
            for part, value in src_ew_fills:
                sp.dma_start(part, value).then_inc(s_pad, 16)
            sp.dma_start(ea_t.rearrange("r (e a) -> (r e) a", a=ED)[0:E, :], ea).then_inc(s_pade, 16)
            for part, value in attr_fills:
                sp.dma_start(part, value).then_inc(s_pade, 16)
            for l in range(3):
                sp.dma_start(by_partition(table[l])[:, W, :], zeros[:, :]).then_inc(s_tab[l], 16)
            sp.wait_ge(s_order, 1)
            sp.dma_start(tile_dst.bitcast(i32), dst_t.rearrange("(b p) e -> p b e", p=P)).then_inc(s_tdst, 16)
            sp.wait_ge(s_toff, 2)
            sp.dma_start(win_d.rearrange("(b p) a -> p b a", p=P), wofi[:, :].unsqueeze(2),
                         allow_slow_non_contiguous=True).then_inc(s_pw, 16)
            sp.wait_ge(s_loc, 1)
            sp.dma_start(loc_p.rearrange("(b p) e -> p b e", p=P), rows_locb).then_inc(s_pw, 16)
            sp.wait_ge(s_pw, 32)
            sp.dma_start(win[:, :], win_d.rearrange("r a -> a r")).then_inc(s_win, 16)
            for b in range(PB):
                sp.wait_ge(s_eag[b % 2], 16 * (b // 2 + 1))
                sp.dma_start(ea_p[b * P:(b + 1) * P, :], rows_ea[:, b % 2, :]).then_inc(s_eaw[b % 2], 16)
            sp.wait_ge(s_srcf, 1)
            sp.dma_start(src_p.rearrange("(b p) e -> p b e", p=P), rows_srcf).then_inc(s_pw, 16)
            sp.wait_ge(s_h, 1)
            sp.dma_start(by_partition(table[0])[:, 0:W, :], H).then_inc(s_tab[0], 16)
            sp.wait_ge(s_pta, 2 * ((PB + 3) // 4))
            sp.dma_start(ew_pc, ew_cols).then_inc(s_ewp, 16)
            for k in range(TABLES):
                sp.wait_ge(s_add, 16 + (k + 1) * (PC // TABLES))
                sp.dma_start(by_partition(sums[k]), zeros[:, :].unsqueeze(1).broadcast_to([P, W1, F])).then_inc(s_zero, 16)
            sp.wait_ge(s_pw, 48)
            sp.wait_ge(s_z, 1)
            sp.dma_start(winrow, win_d.rearrange("r a -> a r").broadcast_to([P, PC])).then_inc(s_wrow, 16)
            sp.wait_ge(s_h, 2)
            sp.dma_start(by_partition(table[1])[:, 0:W, :], H).then_inc(s_tab[1], 16)
            sp.wait_ge(s_att, 1)
            for u in range(2):
                sp.wait_ge(s_eaw[u], 16 * len(range(u, PB, 2)))

            def load_attention(i, u):
                sp.wait_ge(s_mem, i + CH * u + CH)
                rows = loc_p[bass.ds(i + CH * u, CH), :].rearrange("(a j) e -> a (j e)", a=1)
                sp.dma_start(locrow[:, u, :], rows.broadcast_to([P, CH * P])).then_inc(s_lr[u], 2 * CH)
                for h in range(0, CH, CH // 2):
                    sp.wait_ge(s_use, PC + i + CH * u + h + CH // 2)
                    sp.dma_start(G_att[u][:, h:h + CH // 2, F + 1:FX],
                                 ea_p[bass.ds(i + CH * u + h, CH // 2), :].rearrange("j (e a) -> e j a", a=ED)
                                 ).then_inc(s_ea[2 * u + 2 * h // CH], 2 * CH)

            loop(sp, load_attention, PC)
            sp.wait_ge(s_acc, PC)
            sp.wait_ge(s_ewp, 16)
            sp.dma_start(aux_c[:, :], ew_pc).then_inc(s_aux, 16)
            sp.wait_ge(s_h, 3)

            def load_src_rows(i, u):
                sp.wait_ge(s_m2, i + CH * u + CH)
                rows = src_p[bass.ds(i + CH * u, CH), :].rearrange("(a j) e -> a (j e)", a=1)
                sp.dma_start(srcrow[:, u, :], rows.broadcast_to([P, CH * P])).then_inc(s_sr[u], 2 * CH)

            loop(sp, load_src_rows, PC)
            for k in range(TABLES):
                sp.wait_ge(s_sc[k], 16 * PC // TABLES)
            sp.wait_ge(s_y, 16 + PC)
            for b, (w0_, n) in enumerate(BLK):
                if b >= 2:
                    sp.wait_ge(s_tr, 4 * NB + b - 1)
                for k in range(TABLES):
                    sp.dma_start(blkbuf[:, b % 2, k, 0:n, :],
                                 by_partition(sums[k])[:, w0_:w0_ + n, :]).then_inc(s_bl[b % 2], 16)
            sp.wait_ge(s_h, 4)
            sp.dma_start(by_partition(table[2])[:, 0:W, :], H).then_inc(s_tab[2], 16)
            sp.wait_ge(s_moc, 5 * NB)
            sp.dma_start(out[0:FULL * P, :].rearrange("(w p) f -> p w f", p=P), X[:, 0:FULL, :]).then_inc(s_out, 16)
            sp.dma_start(out[FULL * P:N, :], X[0:REST, FULL, :]).then_inc(s_out, 16)
            sp.wait_ge(s_out, 32)

        @block.gpsimd
        def _(pool):
            pool.iota(iota_i[:, :], [[1, P]], base=0, channel_multiplier=0).then_inc(s_iota, 1)
            pool.iota(iota_p[:, :], [[0, 1]], base=0, channel_multiplier=1).then_inc(s_iota, 1)
            pool.wait_ge(s_place, 1)
            with pool.If(load_flag(ENG.Pool) > 0):
                pool.wait_ge(s_pad, PADS)
                pool.wait_ge(s_pade, ATTR_PADS)
                for o, t in ((src_l, src_t), (ew_l, ew_t)):
                    pool.dma_start(o, t.rearrange("r e -> (r e)").rearrange("(p c) -> p c", p=P)).then_inc(s_linb, 16)
                pool.dma_start(ea_p, ea_t).then_inc(s_copy, 16)
                pool.wait_ge(s_linb, 32)
                pool.wait_ge(s_copy, 16)
                with pool.Fori(0, PC - CH + 1, CH) as c:
                    linear_attr = ea_p.rearrange("r (e a) -> (r e) a", a=ED).rearrange("(p c) a -> p c a", p=P)
                    pool.dma_start(attr_s, linear_attr[:, bass.ds(c, CH), :]).then_inc(s_stage, CH)
                    for o, a in ((place_s, place), (src_s, src_l), (dst_s, dst_l), (ew_s, ew_l)):
                        nc.gpsimd.tensor_copy(o, a[:, bass.ds(c, CH)]).then_inc(s_take, CH // 4)
                    pool.wait_ge(s_stage, c + CH)
                    pool.wait_ge(s_take, c + CH)
                    pool.sem_inc(s_taken, 1)
                    for j in range(CH):
                        at_place = bass.IndirectOffsetOnAxis(ap=place_s[:, j:j + 1], axis=0)
                        for t, a in ((dst_t.rearrange("r (e a) -> (r e) a", a=1), dst_s[:, j:j + 1]),
                                     (src_t.rearrange("r (e a) -> (r e) a", a=1), src_s[:, j:j + 1]),
                                     (ew_t.rearrange("r (e a) -> (r e) a", a=1), ew_s[:, j:j + 1]),
                                     (ea_t.rearrange("r (e a) -> (r e) a", a=ED), attr_s[:, j, :])):
                            pool.indirect_dma_start(out=t, out_offset=at_place, in_=a, in_offset=None).then_inc(s_put, 16)
                    pool.wait_ge(s_put, 64 * c + 64 * CH)
            pool.sem_inc(s_order, 1)
            pool.wait_ge(s_toff, 1)
            pool.sem_inc(s_claim, 1)
            for t, rows, gathered in ((dst_t, rows_dst.bitcast(i32), s_drow), (src_t, rows_src.bitcast(i32), s_rows),
                                      (ew_t, rows_ew, s_rows)):
                if t is src_t:
                    pool.wait_ge(s_pad, PADS)
                    pool.sem_inc(s_claim, 1)
                for b in range(PB):
                    tile = bass.IndirectOffsetOnAxis(ap=toff[:, b:b + 1], axis=0)
                    pool.indirect_dma_start(out=rows[:, b, :], out_offset=None, in_=t, in_offset=tile).then_inc(gathered, 16)
            pool.wait_ge(s_pade, ATTR_PADS)
            for b in range(PB):
                tile = bass.IndirectOffsetOnAxis(ap=toff[:, b:b + 1], axis=0)
                if b == 0:
                    pool.wait_ge(s_ln0, 1)
                if b >= 2:
                    pool.wait_ge(s_eaw[b % 2], 16 * (b // 2))
                pool.indirect_dma_start(out=rows_ea[:, b % 2, :], out_offset=None, in_=ea_t, in_offset=tile).then_inc(s_eag[b % 2], 16)

            def gather(i, u, rows, slots, base):
                if not isinstance(i, int):
                    for q in range(4):
                        pool.wait_ge(s_g[4 * u + q], 2 * base + 2 * i)
                pool.sem_inc(s_claim, 1)
                nc.gpsimd.tensor_copy(idx_f[:, u, :], idx_c[:, bass.ds(i + CH * u, CH)]).then_inc(s_idx, CH)
                for q in range(4):
                    pool.wait_ge(s_use, base + i + CH * u + 4 * q + 4)
                    if q == 0:
                        pool.wait_ge(s_idx, base + i + CH * u + CH)
                    pool.sem_inc(s_claim, 1)
                    for j in range(4 * q, 4 * q + 4):
                        edge = bass.IndirectOffsetOnAxis(ap=idx_f[:, u, j:j + 1], axis=0)
                        pool.indirect_dma_start(out=slots[u][:, j, 0:F], out_offset=None, in_=rows,
                                                in_offset=edge).then_inc(s_g[4 * u + q], 16)

            pool.wait_ge(s_ptd, (PB + 3) // 4)
            pool.wait_ge(s_pta, 2 * ((PB + 3) // 4))
            pool.wait_ge(s_tab[0], 32)
            for u in range(2):
                gather(0, u, table[0], G_plain, 0)
            loop(pool, gather, PC, table[0], G_plain, 0, first=2 * CH)
            pool.wait_ge(s_att, 1)
            pool.wait_ge(s_tab[1], 32)
            loop(pool, gather, PC, table[1], G_att, PC)

            def scatter(i, u):
                for j in range(CH):
                    if j == 0:
                        pool.wait_ge(s_ix2, i + CH * u + CH)
                    if j % 4 == 0:
                        pool.wait_ge(s_yc, i + CH * u + j + 4)
                    if u + j // TABLES > 0 or not isinstance(i, int):
                        pool.wait_ge(s_sc[j % TABLES], (i + CH * u) * (16 // TABLES) + 16 * (j // TABLES))
                    pool.sem_inc(s_clm2, 1)
                    node = bass.IndirectOffsetOnAxis(ap=idx_f[:, u, j:j + 1], axis=0)
                    pool.indirect_dma_start(out=sums[j % TABLES], out_offset=node, in_=ysc[:, u, j, :],
                                            in_offset=None, compute_op=ALU.add).then_inc(s_sc[j % TABLES], 16)

            pool.sem_inc(s_clm2, 32)
            pool.wait_ge(s_zero, 16 * TABLES)
            for u in range(2):
                scatter(0, u)
            loop(pool, scatter, PC, first=2 * CH)
            pool.wait_ge(s_tab[2], 32)
            loop(pool, gather, PC, table[2], G_plain, 2 * PC)

        @block.vector
        def _(v):
            steps = [0]

            def step(ins):
                steps[0] += 1
                ins.then_inc(s_d, 1)
                v.wait_ge(s_d, steps[0])

            def tt(o, a, b, op):
                return v.tensor_tensor(o, a, b, op)

            def ts(o, a, s1, s2, op0, op1=ALU.bypass):
                return v.tensor_scalar(o, a, s1, s2, op0, op1)

            def reduce(o, a, op=ALU.add):
                return v.tensor_reduce(out=o, in_=a, op=op, axis=AX.X)

            v.wait_ge(s_iota, 2)
            step(v.tensor_copy(iota[:, :], iota_i[:, :]))
            step(v.tensor_copy(row[:, :], iota_p[:, :]))
            step(v.memset(ones[:, :], 1.0))
            step(v.memset(ones_b[:, :], 1.0))
            step(v.memset(zeros[:, :], 0.0))
            step(v.memset(far[:, :], FAR))
            step(v.memset(att[:, :, :], 0.0))
            step(v.memset(X[:, FULL, :], 0.0))
            step(ts(ident[:, :], iota[:, :], row[:, 0:1], None, ALU.is_equal))
            step(v.tensor_copy(ident_b[:, :], ident[:, :]))
            step(ts(lower[:, :], iota[:, :], row[:, 0:1], None, ALU.is_lt))
            step(ts(thr, iota[:, 0:K1], 1.0, float(P), ALU.add, ALU.mult))
            step(ts(dump[:, :], row[:, :], float(W1), float(W), ALU.mult, ALU.add))
            step(ts(pair, iota[:, 0:PB], float(P), row[:, 0:1], ALU.mult, ALU.add))
            v.sem_inc(s_const, 1)

            def layer_norm(l):
                mean, var, dev, inv = (lns[:, k, :] for k in range(4))
                step(reduce(mean, X[:, :, :]))
                step(ts(mean, mean, 1.0 / F, None, ALU.mult))
                step(tt(H, X[:, :, :], mean.unsqueeze(2).broadcast_to([P, W, F]), ALU.subtract))
                v.sem_inc(s_lnc, 1)
                v.wait_ge(s_lnq, l + 1)
                step(reduce(var, HT[:, 0:NP].rearrange("p (w f) -> p w f", f=F)))
                step(ts(var, var, 1.0 / F, LN_EPS, ALU.mult, ALU.add))
                v.sem_inc(s_lnv, 1)
                v.wait_ge(s_lns, l + 1)
                step(v.reciprocal(inv, dev))
                step(v.scalar_tensor_tensor(H, H, 0.0, inv.unsqueeze(2).broadcast_to([P, W, F]), ALU.max, ALU.mult))

            v.wait_ge(s_lin, 32)
            step(tt(mask, dst_l, next_l, ALU.is_gt))
            step(reduce(order, mask, ALU.max))
            v.sem_inc(s_cmp, 1)
            step(ts(upper, iota[:, :], row[:, 0:1], None, ALU.is_gt))
            step(v.memset(R2[:, P:P + 2 * W1], 0.0))
            v.wait_ge(s_cmps, 1)
            step(v.tensor_copy(unordered[:, :], psum[:, 7, 0:1]))

            def placing(base, k, m):
                n = [0]

                def do(ins):
                    n[0] += 1
                    ins.then_inc(s_vp, 1)
                    v.wait_ge(s_vp, base + k * m + n[0])

                return do

            with v.If(load_flag(ENG.DVE) > 0):
                do = placing(0, 0, 0)
                do(ts(next_l, dst_l, P.bit_length() - 1, None, ALU.logical_shift_right))
                do(v.tensor_copy(hi, next_l))
                do(ts(hi, hi, float(W), None, ALU.min))
                do(v.memset(number, 0.0))
                do(v.memset(total, 0.0))
                with v.Fori(0, W1, 1) as k:
                    do = placing(5, k, 6)
                    do(ts(mask, hi, number, None, ALU.is_equal))
                    do(reduce(count, mask))
                    do(v.tensor_copy(in_window[:, bass.ds(k, 1)], count))
                    do(v.tensor_copy(before_window[:, bass.ds(k, 1)], total))
                    do(tt(total, total, count, ALU.add))
                    do(ts(number, number, 1.0, None, ALU.add))
            v.sem_inc(s_cw, 1)
            v.wait_ge(s_cws, 1)
            with v.If(load_flag(ENG.DVE) > 0):
                do = placing(5 + 6 * W1, 0, 0)
                do(v.tensor_copy(starts, psum[:, 7, 0:W1]))
                do(v.memset(number, 0.0))
                do(v.memset(placef, 0.0))
                with v.Fori(0, W1, 1) as k:
                    do = placing(8 + 6 * W1, k, 7)
                    do(ts(mask, hi, number, None, ALU.is_equal))
                    do(v.tensor_tensor_scan(ranks, mask, mask, 0.0, ALU.add, ALU.bypass))
                    do(v.tensor_copy(start, starts[:, bass.ds(k, 1)]))
                    do(ts(start, start, -1.0, None, ALU.add))
                    do(v.scalar_tensor_tensor(ranks, ranks, start, mask, ALU.add, ALU.mult))
                    do(tt(placef, placef, ranks, ALU.add))
                    do(ts(number, number, 1.0, None, ALU.add))
                do = placing(8 + 13 * W1, 0, 0)
                do(v.tensor_copy(place, placef))
            v.sem_inc(s_place, 1)

            v.wait_ge(s_tdst, 16)
            step(v.tensor_copy(last, tile_dst.bitcast(i32)[:, :, P - 1]))
            step(tt(cmp_k, last.unsqueeze(1).broadcast_to([P, K1, PB]), thr.unsqueeze(2).broadcast_to([P, K1, PB]), ALU.is_lt))
            step(reduce(cnt_k, cmp_k))
            v.sem_inc(s_cntk, 1)
            v.wait_ge(s_aps, 1)
            step(v.scalar_tensor_tensor(bnd, iota[:, 0:K1], 1.0, psum[:, 7, 0:K1], ALU.add, ALU.add))
            step(tt(cmp_p, bnd.unsqueeze(1).broadcast_to([P, PB, K1]), pair.unsqueeze(2).broadcast_to([P, PB, K1]), ALU.is_le))
            step(reduce(wof, cmp_p))
            step(tt(toff[:, :], pair, wof, ALU.subtract))
            v.sem_inc(s_toff, 1)
            step(v.tensor_copy(wofi[:, :], wof))
            v.sem_inc(s_toff, 1)
            step(ts(negw, wof, -float(P), None, ALU.mult))
            v.wait_ge(s_x, 32)
            layer_norm(0)
            v.sem_inc(s_ln0, 1)
            v.wait_ge(s_drow, 16 * PB)
            step(tt(rows_loc, rows_dst.bitcast(i32), negw.unsqueeze(2).broadcast_to([P, PB, P]), ALU.add))
            step(v.tensor_copy(rows_locb, rows_loc))
            v.sem_inc(s_loc, 1)
            PG = (PB + 3) // 4

            v.wait_ge(s_pta, PG)

            def degree_one_hots(i, u):
                v.wait_ge(s_dm, i + CH * u + CH)
                tt(onehot_b[:, u], loc_c[:, bass.ds(i + CH * u, CH)].unsqueeze(2).broadcast_to([P, CH, P]),
                   iota[:, :].unsqueeze(1).broadcast_to([P, CH, P]), ALU.is_equal).then_inc(s_oh, CH)

            loop(v, degree_one_hots, PC)
            v.wait_ge(s_rows, 16 * 2 * PB)
            window, local = rows_src.bitcast(i32), rows_dst.bitcast(i32)
            step(ts(local, window, P - 1, None, ALU.bitwise_and))
            step(ts(window, window, P.bit_length() - 1, None, ALU.logical_shift_right))
            step(v.scalar_tensor_tensor(rows_srcf, local, float(W1), window, ALU.mult, ALU.add))
            v.sem_inc(s_srcf, 1)
            step(tt(selector, wof.unsqueeze(2).broadcast_to([P, PB, W]), iota[:, 0:W].unsqueeze(1).broadcast_to([P, PB, W]), ALU.is_equal))
            v.sem_inc(s_sel, 1)
            for g in range(PG):
                n = min(4, PB - 4 * g)
                v.wait_ge(s_pt, PG + g + 1)
                v.tensor_copy(idx_c[:, 4 * g * P:(4 * g + n) * P], psum[:, (PG + g) % 8, 0:n * P]).then_inc(s_ptd, 1)
            v.wait_ge(s_deg, 1)
            step(ts(dinv[:, :], psum[:, 4, 0:W], 1.0, None, ALU.add))
            v.sem_inc(s_dg, 1)
            v.wait_ge(s_dgr, 1)
            step(v.reciprocal(dinv[:, :], dinv[:, :]))

            dinv_b = dinv[:, :].unsqueeze(2).broadcast_to([P, W, F])
            step(tt(H, H, dinv_b, ALU.mult))
            v.sem_inc(s_h, 1)
            v.wait_ge(s_win, 16)

            def plain_sums(i, u, base, oh_base):
                v.wait_ge(s_use, base + i + CH * u + CH)
                tt(onehot[:, u], loc_c[:, bass.ds(i + CH * u, CH)].unsqueeze(2).broadcast_to([P, CH, P]),
                   iota[:, :].unsqueeze(1).broadcast_to([P, CH, P]), ALU.is_equal).then_inc(s_oh, CH)
                for q in range(4):
                    w = load_windows(ENG.DVE, i + CH * u + 4 * q, 4)
                    v.wait_ge(s_use, 32 + base + i + CH * u + 4 * q + 4)
                    for j in range(4 * q, 4 * q + 4):
                        v.wait_ge(s_add, 16 + oh_base + i + CH * u + j)
                        rows = ACC[:, bass.ds(w[j - 4 * q], 1), 0:F].rearrange("p a f -> p (a f)")
                        tt(rows, rows, bank4(j // 4)[:, j % 4, :], ALU.add).then_inc(s_add, 1)

            step(v.memset(accflat[:, 0:W * FX], 0.0))
            v.sem_inc(s_add, 16)
            v.wait_ge(s_add, 16)
            loop(v, plain_sums, PC, 0, 0)
            v.wait_ge(s_add, 16 + PC)
            step(tt(ACC[:, :, 0:F], ACC[:, :, 0:F], H, ALU.add))
            step(tt(ACC[:, :, 0:F], ACC[:, :, 0:F], dinv_b, ALU.mult))
            v.sem_inc(s_z, 1)

            def batch_norm(l, use, gamma):
                total, mean, sq, dev, inv = (bns[:, k:k + 1] for k in range(5))
                v.wait_ge(s_moc, (use + 1) * NB)
                step(reduce(total, HT[:, 0:N]))
                step(ts(mean, total, 1.0 / N, None, ALU.mult))
                step(ts(HT[:, 0:N], HT[:, 0:N], mean, None, ALU.subtract))
                v.sem_inc(s_bnc, 1)
                v.wait_ge(s_bnq, l + 1)
                step(ts(dev, sq, 1.0 / N, BN_EPS, ALU.mult, ALU.add))
                v.sem_inc(s_bnv, 1)
                v.wait_ge(s_bns, l + 1)
                step(v.reciprocal(inv, dev))
                step(tt(inv, inv, gamma, ALU.mult))
                v.sem_inc(s_bna, 1)
                for b, (w0_, n) in enumerate(BLK):
                    v.wait_ge(s_bt, l * NB + b + 1)
                    full = n if w0_ + n < W else n - 1
                    if full:
                        o = X[:, w0_:w0_ + full, :]
                        ins = tt(o, o, bank4(4 + b % 2)[:, 0:full, :], ALU.add)
                    if full < n:
                        o = X[0:REST, FULL, :]
                        ins = tt(o, o, bank4(4 + b % 2)[0:REST, full, :], ALU.add)
                    ins.then_inc(s_btc, 1)
                v.wait_ge(s_btc, (l + 1) * NB)

            batch_norm(0, 0, cols[:, 1:2])

            layer_norm(1)
            v.sem_inc(s_h, 1)
            v.wait_ge(s_wrow, 16)
            same_w = R2[:, PC // 2:PC // 2 + PC - 1]
            step(tt(same_w, winrow[:, 1:PC], winrow[:, 0:PC - 1], ALU.is_equal))
            v.wait_ge(s_ewp, 16)
            step(ts(aux_c[:, 1:PC], same_w, -2.0 * NOTHING, NOTHING, ALU.mult, ALU.add))
            step(v.memset(aux_c[:, 0:1], NOTHING))
            for q, (w0_, n) in enumerate(QB):
                v.wait_ge(s_qh, q + 1)
                high = Q3[:, 0, w0_:w0_ + n, :]
                rem = qrem[:, 3 * (q % 2):3 * (q % 2) + n, :]
                step(tt(rem, psum[:, 4 + q % 2, 0:n * FX].rearrange("p (w f) -> p w f", f=FX), high, ALU.subtract))
                v.sem_inc(s_qs, 1)
                step(v.tensor_copy(Q3[:, 1, w0_:w0_ + n, :], rem))
                step(tt(Q3[:, 2, w0_:w0_ + n, :], rem, Q3[:, 1, w0_:w0_ + n, :], ALU.subtract))
            step(v.memset(accflat[:, 0:W * FX], 0.0))
            v.wait_ge(s_tab[1], 32)
            v.wait_ge(s_trc, 2 * NB)
            for u in range(2):
                step(v.memset(G_att[u][:, :, F:F + 1], 1.0))
            step(tt(picks[:, :], ident[:, 0:GR], ident[:, GR:2 * GR], ALU.add))
            step(tt(picks[:, :], picks[:, :], ident[:, 2 * GR:3 * GR], ALU.add))
            step(v.tensor_copy(pick, picks[0:3 * GR, :].unsqueeze(2).broadcast_to([3 * GR, GR, P])))
            v.sem_inc(s_att, 1)
            v.sem_inc(s_mem, 32)
            score, oldm, newm, corr = (att[:, k, :] for k in range(4))

            windows = [None]

            def attention_vector(i, k):
                p = i + k
                if (k + 4) % CH == 0 and there(i, k + 4):
                    u = ((k + 4) // CH) % 2
                    v.wait_ge(s_lr[u], p + 4 - CH * u + 2 * CH)
                    if there(i, k - 13):
                        v.wait_ge(s_min, p - 12)
                    ts(member[:, u], pairs(locrow[:, u, :]), row[:, 0:1], None, ALU.is_equal)
                    ts(penalty[:, u], pairs(locrow[:, u, :]), row[:, 0:1], MASKED, ALU.not_equal, ALU.mult)
                    v.tensor_copy(col_f[:, u, 0, :], aux_c[:, bass.ds(p + 4, CH)]).then_inc(s_mem, CH)
                if there(i, k):
                    v.wait_ge(s_qe, p + 2)
                for j in range(2):
                    if there(i, k - 12):
                        a, u = (k - 12 + j) % CH, ((k - 12 + j) // CH) % 2
                        if peeled(i) and j == 0:
                            v.wait_ge(s_row, p - 10)
                            if there(i, k - 20):
                                v.wait_ge(s_et, p - 18)
                        v.wait_ge(s_min, p - 12 + j)
                        if a == 0:
                            v.wait_ge(s_mem, 32 + p - 12 + CH)
                        v.tensor_tensor(oldm[:, a:a + 1], newm[:, (a - 1) % CH:(a - 1) % CH + 1],
                                        col_f[:, u, 0, a:a + 1], ALU.max).then_inc(s_nmo, 1)
                    if there(i, k - 20):
                        if j == 0 and k == LAST:
                            windows[0] = load_windows(ENG.DVE, p - 20, 4)
                        b = (k - 20 + j) % CH
                        if peeled(i):
                            v.wait_ge(s_use, PC + 32 + p - 18)
                            v.wait_ge(s_acc, p - 20 + j)
                            v.wait_ge(s_c, p - 19 + j)
                        rows = ACC[:, bass.ds(windows[0][(k - 20 + j) % 4], 1), :].rearrange("p a f -> p (a f)")
                        v.scalar_tensor_tensor(rows, rows, corr[:, b:b + 1], two(6, k - 20 + j, FX), ALU.mult,
                                               ALU.add).then_inc(s_acc, 1)
                    g = (k // GR) % 2
                    if k % GR == 0 and there(i, k - 4) and j == 1:
                        v.wait_ge(s_shi, p)
                        o = (k - 4) % CH
                        tt(rem_s[:, 1 - g, :], score[:, o:o + GR], parts[:, 1 - g, 0:GR], ALU.subtract).then_inc(s_srem, GR)
                    if k % GR == 2 and there(i, k - 6) and j == 1:
                        v.wait_ge(s_smid, p - 2)
                        tt(parts[:, 1 - g, 2 * GR:3 * GR], rem_s[:, 1 - g, :], parts[:, 1 - g, GR:2 * GR],
                           ALU.subtract).then_inc(s_slo, GR)
                    if there(i, k - 12):
                        v.wait_ge(s_nmo, p - 11 + j)
                        v.sem_inc(s_vclaim, 1)
                        v.tensor_tensor_reduce(out=masked[:, (k - 12 + j) % 8, :], in0=two(2, k - 12 + j, P),
                                               in1=penalty[:, u, a, :], scale=1.0, scalar=oldm[:, a:a + 1],
                                               op0=ALU.add, op1=ALU.min, accum_out=newm[:, a:a + 1]).then_inc(s_min, 1)
                    if there(i, k):
                        s = k % 32 + j
                        if s % 4 == 0:
                            v.wait_ge(s_g[s // 4], 2 * PC + 2 * (p + j - s) + 64)
                        if s % (CH // 2) == 0:
                            v.wait_ge(s_ea[s // (CH // 2)], p + j - s + 32)
                        if peeled(i) and there(i, k + j - 2):
                            v.wait_ge(s_dot, p + j - 1)
                        v.tensor_tensor_reduce(out=junk[:, j, :], in0=two(0, k + j, FX),
                                               in1=G_att[s // CH][:, s % CH, :], scale=1.0, scalar=0.0, op0=ALU.mult,
                                               op1=ALU.add, accum_out=score[:, s % CH:s % CH + 1]).then_inc(s_dot, 1)
                    if k % 4 == 2 and j == 0 and k != LAST - 2 and there(i, k - 18):
                        ahead = load_windows(ENG.DVE, p - 18, 4)
                    if k % 4 == 2 and j == 1 and k != LAST - 2 and there(i, k - 18):
                        windows[0] = ahead

            attention(v, attention_vector)
            v.wait_ge(s_acc, PC)
            den = lns[:, 0, :]
            step(ts(den, ACC[:, :, F], 1.0e-37, None, ALU.max))
            step(v.reciprocal(den, den))
            step(tt(ACC, ACC, den.unsqueeze(2).broadcast_to([P, W, FX]), ALU.mult))
            v.sem_inc(s_agn, 1)
            batch_norm(1, 2, cols[:, 5:6])

            layer_norm(2)
            v.sem_inc(s_h, 1)
            v.sem_inc(s_m2, 32)
            v.wait_ge(s_aux, 16)
            v.sem_inc(s_small, CH)

            def combine_vector(i, u):
                p0 = i + CH * u
                idx = idx_c[:, bass.ds(p0, CH)]
                locf, ewf, idf = (col_f[:, u, k, :] for k in range(3))
                v.wait_ge(s_cm, p0 + CH)
                v.tensor_copy(locf, loc_c[:, bass.ds(p0, CH)])
                v.tensor_copy(ewf, aux_c[:, bass.ds(p0, CH)])
                v.tensor_copy(idf, idx).then_inc(s_col, CH)
                v.wait_ge(s_sr[u], i + 2 * CH)
                v.wait_ge(s_col, p0 + CH)
                tt(same[:, u], pairs(srcrow[:, u, :]), idf.unsqueeze(2).broadcast_to([P, CH, P]), ALU.is_equal).then_inc(s_same, CH)
                for j in range(CH):
                    v.tensor_scalar(onehot[:, u, j, :], iota[:, :], locf[:, j:j + 1], ewf[:, j:j + 1],
                                    ALU.is_equal, ALU.mult).then_inc(s_m2, 1)
                v.wait_ge(s_same, p0 + CH)
                v.wait_ge(s_small, CH + 4 * p0)
                tt(earlier, same[:, u], lower[:, :].unsqueeze(1).broadcast_to([P, CH, P]), ALU.mult).then_inc(s_ear, CH)
                v.wait_ge(s_ear, p0 + CH)
                reduce(dup, earlier).then_inc(s_small, CH)
                v.wait_ge(s_small, 4 * p0 + 2 * CH)
                ts(dup, dup, 1.0, None, ALU.min).then_inc(s_small, CH)
                ts(tgt, idf, -1.0, dump[:, 0:1], ALU.mult, ALU.add).then_inc(s_small, CH)
                v.wait_ge(s_small, 4 * p0 + 4 * CH)
                tt(tgt, tgt, dup, ALU.mult).then_inc(s_small, CH)
                v.wait_ge(s_small, 4 * p0 + 5 * CH)
                v.wait_ge(s_clm2, p0 + 24)
                tt(idx_f[:, u, :], tgt, idf, ALU.add).then_inc(s_ix2, CH)

            dup, tgt = att[:, 0, :], att[:, 1, :]
            loop(v, combine_vector, PC)

            def add_blocks(use):
                for b, (w0_, n) in enumerate(BLK):
                    v.wait_ge(s_mo, use * NB + b + 1)
                    o = X[:, w0_:w0_ + n, :]
                    tt(o, o, bank4(2 + b % 2)[:, 0:n, :], ALU.add).then_inc(s_moc, 1)
                v.wait_ge(s_moc, (use + 1) * NB)

            add_blocks(3)
            layer_norm(3)
            v.sem_inc(s_h, 1)
            step(v.memset(accflat[:, 0:W * FX], 0.0))
            loop(v, plain_sums, PC, 2 * PC, PC)
            v.wait_ge(s_add, 16 + 2 * PC)
            v.sem_inc(s_z, 1)
            add_blocks(4)

        @block.tensor
        def _(t):
            def mm(o, lhs_t, rhs, start=True, stop=True):
                return nc.tensor.matmul(o, lhs_t, rhs, start=start, stop=stop)

            t.wait_ge(s_w, WEIGHTS)
            t.wait_ge(s_const, 1)
            for k, m in enumerate((1, 2, 3, 4)):
                nc.tensor.transpose(bank4(6)[:, k, :], Wm[:, m, :], ident[:, :])
            nc.tensor.transpose(psum[0:X1, 5, 0:P], VX[:, :], ident[:, :]).then_inc(s_wt, 1)
            t.wait_ge(s_cmp, 1)
            mm(psum[:, 7, 0:1], ones[:, :], order).then_inc(s_cmps, 1)
            t.wait_ge(s_cw, 1)
            mm(psum[:, 7, 0:W1], upper, in_window, stop=False)
            mm(psum[:, 7, 0:W1], ones[:, :], before_window, start=False).then_inc(s_cws, 1)
            t.wait_ge(s_cntk, 1)
            mm(psum[:, 7, 0:K1], ones[:, :], cnt_k).then_inc(s_aps, 1)
            PG = (PB + 3) // 4
            t.wait_ge(s_loc, 1)
            t.wait_ge(s_wtc, 1)

            def to_columns(a, rows):
                for g in range(PG):
                    n = min(4, PB - 4 * g)
                    for j in range(n):
                        last_ins = nc.tensor.transpose(bank4((a * PG + g) % 8)[:, j, :], rows[:, 4 * g + j, :], ident[:, :])
                    last_ins.then_inc(s_pt, 1)

            assert PG <= 4
            to_columns(0, rows_loc)
            t.sem_inc(s_dm, 32)
            t.wait_ge(s_pta, PG)

            def count_degrees(i, u):
                t.wait_ge(s_oh, i + CH * u + CH)
                t.wait_ge(s_dmc, i + CH * u + CH)
                for j in range(CH):
                    mm(psum[:, u, j:j + 1], onehot_b[:, u, j, :], ones_b[:, :]).then_inc(s_dm, 1)

            loop(t, count_degrees, PC)
            t.wait_ge(s_dmc, 32 + PC)
            for g in range(PG):
                n = min(4, PB - 4 * g)
                for j in range(n):
                    b = 4 * g + j
                    last_ins = nc.tensor.transpose(bank4(g % 4)[:, j, :], counts[:, b * P:(b + 1) * P], ident[:, :])
                last_ins.then_inc(s_ct, 1)
            t.wait_ge(s_srcf, 1)
            t.wait_ge(s_ctc, PG)
            to_columns(1, rows_srcf)
            t.wait_ge(s_ptd, PG)
            t.wait_ge(s_sel, 1)
            for b in range(PB):
                last_ins = mm(psum[:, 4, 0:W], counts_t[:, b, :], selector[:, b, :], start=b == 0, stop=b == PB - 1)
            last_ins.then_inc(s_deg, 1)
            t.wait_ge(s_dg, 1)
            to_columns(2, rows_ew)
            t.wait_ge(s_pta, 2 * PG)

            def plain_products(i, u, base, add_base):
                t.wait_ge(s_oh, PC + add_base + i + CH * u + CH)
                for q in range(4):
                    t.wait_ge(s_g[4 * u + q], 2 * base + 2 * i + 64)
                    t.wait_ge(s_add, add_base + i + CH * u + 4 * q + 4)
                    for j in range(4 * q, 4 * q + 4):
                        mm(bank4(j // 4)[:, j % 4, :], onehot[:, u, j, :], G_plain[u][:, j, 0:F]).then_inc(s_use, 1)

            def transposes(use, view, rows=P):
                t.wait_ge(s_trc, use * NB)
                for b, (w0_, n) in enumerate(BLK):
                    if b >= 2:
                        t.wait_ge(s_trc, use * NB + b - 1)
                    for j in range(n):
                        last_ins = nc.tensor.transpose(bank4(b % 2)[0:rows, j, :], view(w0_ + j), ident[:, :])
                    last_ins.then_inc(s_tr, 1)

            def products(use, emit):
                t.wait_ge(s_moc, use * NB)
                for b, (w0_, n) in enumerate(BLK):
                    if b >= 2:
                        t.wait_ge(s_moc, use * NB + b - 1)
                    emit(2 + b % 2, w0_, n).then_inc(s_mo, 1)

            def transposes_back(l):
                t.wait_ge(s_bn, l + 1)
                for b, (w0_, n) in enumerate(BLK):
                    if b >= 2:
                        t.wait_ge(s_btc, l * NB + b - 1)
                    for j in range(n):
                        w = w0_ + j
                        m = min(P, N - w * P)
                        last_ins = nc.tensor.transpose(bank4(4 + b % 2)[0:m, j, :], HT[:, w * P:w * P + m], ident[:, :])
                    last_ins.then_inc(s_bt, 1)

            t.sem_inc(s_use, 32)
            loop(t, plain_products, PC, 0, 0)
            t.wait_ge(s_z, 1)
            transposes(0, lambda w: ACC[:, w, 0:F])
            t.wait_ge(s_trc, NB)
            products(0, lambda bank, w, n: mm(psum[:, bank, 0:n * P], Wm[:, 0, :], HT[:, w * P:(w + n) * P]))
            transposes_back(0)
            t.wait_ge(s_h, 2)
            t.wait_ge(s_btc, NB)
            transposes(1, lambda w: H[:, w, :])
            t.wait_ge(s_trc, 2 * NB)
            products(1, lambda bank, w, n: mm(psum[:, bank, 0:n * P], WT[:, 0, :], HT[:, w * P:(w + n) * P]))
            t.wait_ge(s_moc, 2 * NB)
            for q, (w0_, n) in enumerate(QB):
                if q >= 2:
                    t.wait_ge(s_qs, q - 1)
                for j in range(n):
                    last_ins = mm(psum[:, 4 + q % 2, j * FX:(j + 1) * FX], QT[:, (w0_ + j) * P:(w0_ + j + 1) * P], C[:, :])
                last_ins.then_inc(s_q, 1)
            t.wait_ge(s_att, 1)
            score = att[:, 0, :]

            windows = [None]

            def attention_tensor(i, k):
                p = i + k
                if there(i, k - 18):
                    t.wait_ge(s_etc, p - 16)
                    if there(i, k - 22):
                        t.wait_ge(s_acc, p - 20)
                    for s in ((k - 18) % 32, (k - 18) % 32 + 1):
                        mm(two(6, s, FX), ET[:, s % 4, :], G_att[s // CH][:, s % CH, :]).then_inc(s_use, 1)
                if k % GR == 2 and there(i, k - 10):
                    t.wait_ge(s_stc, p - 6)
                if there(i, k - 16):
                    t.wait_ge(s_exp, p - 14)
                    if peeled(i) and there(i, k - 20):
                        t.wait_ge(s_etc, p - 18)
                    for q in (k - 16, k - 15):
                        nc.tensor.transpose(two(4, q, P), masked[:, q % 8, :], ident[:, :]).then_inc(s_et, 1)
                if k % GR == 0 and there(i, k - 8):
                    t.wait_ge(s_slo, p - 4)
                    if peeled(i) and there(i, k - 18):
                        t.wait_ge(s_etc, p - 16)
                    nc.tensor.transpose(rows_ps, parts[:, k // GR % 2, :], ident_b[:, :]).then_inc(s_str, GR)
                if there(i, k - 2):
                    t.wait_ge(s_dot, p)
                if there(i, k - 10):
                    if peeled(i) and there(i, k - 14):
                        t.wait_ge(s_min, p - 12)
                    for q in (k - 10, k - 9):
                        mm(two(2, q, P), pick[:, q % GR, :], ST[:, q // GR % 2, :]).then_inc(s_row, 1)
                if there(i, k + 2):
                    s0 = (k + 2) % 32
                    if k == LAST:
                        windows[0] = load_windows(ENG.PE, p, 4)
                    if s0 % CH == 0:
                        t.wait_ge(s_mem, 32 + p + 2 + CH)
                    for s in (s0, s0 + 1):
                        for part in range(3):
                            ins = mm(two(0, s, FX), member[:, s // CH, s % CH, :],
                                     Q3[:, part, bass.ds(windows[0][s % 4], 1), :].rearrange("p a f -> p (a f)"),
                                     start=part == 0, stop=part == 2)
                        ins.then_inc(s_qe, 1)
                if k % 4 == 0 and there(i, k + 4):
                    windows[0] = load_windows(ENG.PE, p + 4, 4)

            attention(t, attention_tensor)
            t.wait_ge(s_agn, 1)
            transposes(2, lambda w: ACC[:, w, 0:F])
            transposes(3, lambda w: ACC[:, w, F:FX], rows=X1)
            t.wait_ge(s_trc, 4 * NB)

            def attention_out(bank, w, n):
                nodes = slice(w * P, (w + n) * P)
                o = psum[:, bank, 0:n * P]
                mm(o, WT[:, 1, :], AGT[:, nodes], stop=False)
                mm(o, VXT[:, :], EXT[:, nodes], start=False, stop=False)
                return mm(o, WT[:, 2, :], HT[:, nodes], start=False)

            products(2, attention_out)
            transposes_back(1)
            t.wait_ge(s_h, 3)
            t.wait_ge(s_btc, 2 * NB)
            t.sem_inc(s_cm, 32)
            t.sem_inc(s_y, 16)

            def combine_tensor(i, u):
                p0 = i + CH * u
                for q in range(4):
                    w = load_windows(ENG.PE, p0 + 4 * q, 4)
                    t.wait_ge(s_m2, 32 + p0 + 4 * q + 4)
                    t.wait_ge(s_cmc, p0 + 4 * q + 4)
                    for j in range(4 * q, 4 * q + 4):
                        mm(bank4(q)[:, j % 4, :], onehot[:, u, j, :], same[:, u, j, :]).then_inc(s_cm, 1)
                    t.wait_ge(s_cmc, 16 + p0 + 4 * q + 4)
                    for j in range(4 * q, 4 * q + 4):
                        mm(bank4(4 + q)[:, j % 4, :], cmb[:, j, :],
                           H[:, bass.ds(w[j - 4 * q], 1), :].rearrange("p a f -> p (a f)")).then_inc(s_y, 1)

            loop(t, combine_tensor, PC)
            t.wait_ge(s_trc, 4 * NB)
            for b, (w0_, n) in enumerate(BLK):
                t.wait_ge(s_bl[b % 2], 16 * TABLES * (b // 2 + 1))
                if b >= 2:
                    t.wait_ge(s_trc, 4 * NB + b - 1)
                for j in range(n):
                    for k in range(TABLES):
                        last_ins = mm(bank4(b % 2)[:, j, :], blkbuf[:, b % 2, k, j, :], ident[:, :], start=k == 0, stop=k == TABLES - 1)
                last_ins.then_inc(s_tr, 1)
            t.wait_ge(s_trc, 5 * NB)

            def scattered_out(bank, w, n):
                for j in range(n):
                    o = bank4(bank)[:, j, :]
                    mm(o, HT[:, (w + j) * P:(w + j + 1) * P], WT[:, 3, :], stop=False)
                    ins = mm(o, ones[0:1, :], b2row[:, :], start=False)
                return ins

            products(3, scattered_out)
            loop(t, plain_products, PC, 2 * PC, PC)
            t.wait_ge(s_z, 2)
            transposes(5, lambda w: ACC[:, w, 0:F])
            transposes(6, lambda w: H[:, w, :])
            t.wait_ge(s_trc, 7 * NB)

            def plain_out(bank, w, n):
                for j in range(n):
                    o = bank4(bank)[:, j, :]
                    mm(o, HT[:, (w + j) * P:(w + j + 1) * P], Wm[:, 5, :], stop=False)
                    ins = mm(o, H3T[:, (w + j) * P:(w + j + 1) * P], Wm[:, 6, :], start=False)
                return ins

            products(4, plain_out)

        @block.scalar
        def _(act):
            def activation(o, a, f, **kw):
                return nc.scalar.activation(o, a, f, **kw)

            for k, m in enumerate((w0, wq, wv, wskip, w2, w3, wself)):
                act.dma_start(Wm[:, k, :], m).then_inc(s_w, 16)
            act.dma_start(C[:, 0:F], wk).then_inc(s_w, 16)
            for o, m in ((C[:, F:F + 1], bk), (VX[:, 0:1], bv), (cols[:, 0:1], b0), (cols[:, 1:2], g0),
                         (cols[:, 2:3], be0), (cols[:, 3:4], bq), (cols[:, 4:5], bskip), (cols[:, 5:6], g1),
                         (cols[:, 6:7], be1)):
                act.dma_start(o, m.rearrange("(p a) -> p a", a=1)).then_inc(s_w, 16)
            act.dma_start(C[:, F + 1:FX], we).then_inc(s_w, 16)
            act.dma_start(VX[:, 1:X1], we).then_inc(s_w, 16)
            act.dma_start(b2row[:, :], b2.rearrange("(a n) -> a n", a=1)).then_inc(s_w, 16)
            act.wait_ge(s_w, WEIGHTS)
            act.wait_ge(s_wt, 1)
            activation(cols[:, 7:8], cols[:, 3:4], ACT.Copy, scale=-SCALE)
            activation(VXT[:, :], psum[0:X1, 5, 0:P], ACT.Copy)
            activation(WT[:, :, :], bank4(6), ACT.Copy).then_inc(s_wtc, 1)

            def layer_norm(l):
                act.wait_ge(s_lnc, l + 1)
                activation(HT[:, 0:NP], hflat[:, 0:NP], ACT.Square).then_inc(s_lnq, 1)
                act.wait_ge(s_lnv, l + 1)
                activation(lns[:, 2, :], lns[:, 1, :], ACT.Sqrt).then_inc(s_lns, 1)

            layer_norm(0)
            PG = (PB + 3) // 4

            def copy_columns(a, o):
                for g in range(PG):
                    n = min(4, PB - 4 * g)
                    act.wait_ge(s_pt, a * PG + g + 1)
                    activation(o[:, 4 * g * P:(4 * g + n) * P], psum[:, (a * PG + g) % 8, 0:n * P], ACT.Copy).then_inc(s_pta, 1)

            copy_columns(0, loc_c[:, :])
            act.sem_inc(s_dmc, 32)

            def copy_counts(i, u):
                act.wait_ge(s_dm, 32 + i + CH * u + CH)
                activation(counts[:, bass.ds(i + CH * u, CH)], psum[:, u, 0:CH], ACT.Copy).then_inc(s_dmc, CH)

            act.wait_ge(s_loc, 1)
            loop(act, copy_counts, PC)
            for g in range(PG):
                n = min(4, PB - 4 * g)
                act.wait_ge(s_ct, g + 1)
                activation(counts_t[:, 4 * g:4 * g + n, :], bank4(g % 4)[:, 0:n, :], ACT.Copy).then_inc(s_ctc, 1)
            act.wait_ge(s_dg, 1)
            activation(dinv[:, :], dinv[:, :], ACT.Sqrt).then_inc(s_dgr, 1)
            copy_columns(2, ew_cols)

            def copy_blocks(use, o, rows=P):
                for b, (w0_, n) in enumerate(BLK):
                    act.wait_ge(s_tr, use * NB + b + 1)
                    activation(o[:, w0_ * P:(w0_ + n) * P], psum[0:rows, b % 2, 0:n * P], ACT.Copy).then_inc(s_trc, 1)

            def use_products(use, o, func, bias, scale=1.0):
                for b, (w0_, n) in enumerate(BLK):
                    act.wait_ge(s_mo, use * NB + b + 1)
                    activation(o[:, w0_ * P:(w0_ + n) * P], psum[:, 2 + b % 2, 0:n * P], func, bias=bias, scale=scale).then_inc(s_moc, 1)

            def batch_norm(l, func, beta, scratch):
                act.wait_ge(s_bnc, l + 1)
                activation(scratch[:, 0:N], HT[:, 0:N], ACT.Square, accum_out=bns[:, 2:3]).then_inc(s_bnq, 1)
                act.wait_ge(s_bnv, l + 1)
                activation(bns[:, 3:4], bns[:, 3:4], ACT.Sqrt).then_inc(s_bns, 1)
                act.wait_ge(s_bna, l + 1)
                activation(HT[:, 0:N], HT[:, 0:N], func, bias=beta, scale=bns[:, 4:5]).then_inc(s_bn, 1)

            copy_blocks(0, HT)
            use_products(0, HT, ACT.Identity, cols[:, 0:1])
            batch_norm(0, ACT.Relu, cols[:, 2:3], hflat)
            layer_norm(1)
            copy_blocks(1, HT)
            use_products(1, QT, ACT.Identity, cols[:, 7:8], -SCALE)
            for q, (w0_, n) in enumerate(QB):
                act.wait_ge(s_q, q + 1)
                activation(Q3[:, 0, w0_:w0_ + n, :], psum[:, 4 + q % 2, 0:n * FX].rearrange("p (w f) -> p w f", f=FX),
                           ACT.Copy).then_inc(s_qh, 1)
            act.wait_ge(s_att, 1)
            score, oldm, newm, corr = (att[:, k, :] for k in range(4))

            def attention_scalar(i, k):
                p = i + k
                g = (k // GR) % 2
                if k % GR == 0 and there(i, k - 4):
                    s = (k - 4) % CH
                    act.wait_ge(s_dot, p)
                    activation(parts[:, 1 - g, 0:GR], score[:, s:s + GR], ACT.Copy).then_inc(s_shi, GR)
                if k % GR == 2 and there(i, k - 6):
                    act.wait_ge(s_srem, p - 2)
                    activation(parts[:, 1 - g, GR:2 * GR], rem_s[:, 1 - g, :], ACT.Copy).then_inc(s_smid, GR)
                if there(i, k - 16):
                    act.wait_ge(s_et, p - 14)
                    if peeled(i) and there(i, k - 20):
                        act.wait_ge(s_use, PC + 32 + p - 18)
                    o = (k - 16) % 4
                    activation(ET[:, o:o + 2, :], bank4(4 + (k - 16) // 2 % 2)[:, 0:2, :], ACT.Copy).then_inc(s_etc, 2)
                if k % GR == 0 and there(i, k - 8):
                    act.wait_ge(s_str, p - 4)
                    if peeled(i) and there(i, k - 14):
                        act.wait_ge(s_row, p - 12)
                    activation(ST[:, g, :], rows_ps, ACT.Copy).then_inc(s_stc, GR)
                if there(i, k - 12):
                    for j in range(2):
                        a = (k - 12 + j) % CH
                        act.wait_ge(s_min, p - 11 + j)
                        e = masked[:, (k - 12 + j) % 8, :]
                        activation(e, e, ACT.Exp, bias=newm[:, a:a + 1], scale=-1.0).then_inc(s_exp, 1)
                        activation(corr[:, a:a + 1], oldm[:, a:a + 1], ACT.Exp, bias=newm[:, a:a + 1],
                                   scale=-1.0).then_inc(s_c, 1)

            attention(act, attention_scalar)
            act.wait_ge(s_agn, 1)
            copy_blocks(2, AGT)
            copy_blocks(3, EXT, rows=X1)
            use_products(2, HT, ACT.Relu, cols[:, 4:5])
            batch_norm(1, ACT.Identity, cols[:, 6:7], AGT)
            layer_norm(2)
            act.wait_ge(s_h, 3)
            act.sem_inc(s_cmc, 16)

            def combine_scalar(i, u):
                p0 = i + CH * u
                for q in range(4):
                    act.wait_ge(s_cm, 32 + p0 + 4 * q + 4)
                    act.wait_ge(s_y, p0 + 4 * q + 4)
                    activation(cmb[:, 4 * q:4 * q + 4, :], bank4(q), ACT.Copy).then_inc(s_cmc, 4)
                    act.wait_ge(s_y, 16 + p0 + 4 * q + 4)
                    act.wait_ge(s_clm2, p0 + 4 * q + 12)
                    activation(ysc[:, u, 4 * q:4 * q + 4, :], bank4(4 + q), ACT.Copy).then_inc(s_yc, 4)

            loop(act, combine_scalar, PC)
            copy_blocks(4, HT)
            layer_norm(3)
            copy_blocks(5, HT)
            copy_blocks(6, H3T)


_INS = ["x", "src", "dst", "edge_attr_10", "edge_weight", "L0_gnn_weight", "L0_gnn_bias", "L0_gnn_gamma",
        "L0_gnn_beta", "L1_gnn_Wq", "L1_gnn_bq", "L1_gnn_Wk", "L1_gnn_bk", "L1_gnn_Wv", "L1_gnn_bv",
        "L1_gnn_We", "L1_gnn_Wskip", "L1_gnn_bskip", "L1_gnn_gamma", "L1_gnn_beta", "L2_gnn_W",
        "L2_gnn_b", "L3_gnn_W", "L3_gnn_W_self"]


def kernel(**inputs):
    import numpy as _np
    import concourse.bacc as _bacc
    from concourse import mybir as _mybir
    from concourse.bass_utils import run_bass_kernel_spmd as _run

    nc = _bacc.Bacc("TRN2", target_bir_lowering=False, num_devices=1)
    arrays, args = {}, []
    for name in _INS:
        a = _np.ascontiguousarray(inputs[name])
        arrays[f"in_{name}_dram"] = a
        args.append(nc.dram_tensor(f"in_{name}_dram", a.shape, _mybir.dt.from_np(a.dtype), kind="ExternalInput").ap())
    shape = inputs["x"].shape
    args.append(nc.dram_tensor("out_0_dram", shape, _mybir.dt.float32, kind="ExternalOutput").ap())
    gnn_kernel(nc, *args)
    r = _run(nc, [arrays], core_ids=[0])
    return r.results[0]["out_0_dram"]
```
